# Optimizing a Trainium2 kernel written in Bass

```python
import numpy as np
import jax
import jax.numpy as jnp

def _softmax(x, axis=-1):
    return jax.nn.softmax(x, axis=axis)

def _gelu(x):
    return jax.nn.gelu(x, approximate=True)

def _silu(x):
    return jax.nn.silu(x)

def _sigmoid(x):
    return jax.nn.sigmoid(x)

def _layernorm(x, axis=-1, eps=1e-05):
    m = jnp.mean(x, axis=axis, keepdims=True)
    v = jnp.var(x, axis=axis, keepdims=True)
    return (x - m) / jnp.sqrt(v + eps)

def _scatter_add(tgt, idx, src, axis=0):
    return tgt.at[idx].add(src)

def _segment_sum(src, seg, n):
    return jax.ops.segment_sum(src, seg, n)
kernel_name = 'mk_cond_resid_d2_seqx_r4_969e3c'

def setup_inputs(seed: int=0):
    np.random.seed(seed)
    _w = jnp.asarray

    def _rec_inputs():
        import jax
        import jax.numpy as jnp
        _rk = jax.random.key(seed)
        x = -0.0005207 + 1.001 * jax.random.normal(jax.random.fold_in(_rk, 1), (2, 1024, 256), jnp.float32)
        _lenS = 1024 - jax.random.randint(jax.random.fold_in(_rk, 7), (2,), 0, max(1, 1024 // 4) + 1, jnp.int32)
        _lenS2 = 1024 - jax.random.randint(jax.random.fold_in(_rk, 8), (2,), 0, max(1, 1024 // 4) + 1, jnp.int32)
        fside_Bx8_0 = jax.random.uniform(jax.random.fold_in(_rk, 11), (2, 8), jnp.float32, 0.0, 0.556406)
        condB_sharedgateprob = jax.random.uniform(jax.random.fold_in(_rk, 12), (2,), jnp.float32, 0.0, 0.794948)
        itok_B_0_2 = jax.random.randint(jax.random.fold_in(_rk, 13), (2,), 0, 3, jnp.int32)
        return (x, fside_Bx8_0, condB_sharedgateprob, itok_B_0_2)
    x, fside_Bx8_0, condB_sharedgateprob, itok_B_0_2 = _rec_inputs()

    def _L0_cond_setup():
        import jax, jax.numpy as jnp
        import numpy as np
        E, B, S, D, F = (8, 2, 256, 256, 1024)
        key = jax.random.key(seed)
        ks = jax.random.split(key, 9)
        sc_d = 1.0 / np.sqrt(D)
        sc_f = 1.0 / np.sqrt(F)
        hidden_states = jax.random.normal(ks[0], (B, S, D), dtype=jnp.float32)
        gating_probs = jax.nn.softmax(jax.random.normal(ks[1], (B, E), dtype=jnp.float32), axis=-1)
        shared_gate_prob = jax.nn.sigmoid(jax.random.normal(ks[2], (B, 1), dtype=jnp.float32))
        Wg = jax.random.normal(ks[3], (E, D, F), dtype=jnp.float32) * sc_d
        Wu = jax.random.normal(ks[4], (E, D, F), dtype=jnp.float32) * sc_d
        Wd = jax.random.normal(ks[5], (E, F, D), dtype=jnp.float32) * sc_f
        Sg = jax.random.normal(ks[6], (D, F), dtype=jnp.float32) * sc_d
        Su = jax.random.normal(ks[7], (D, F), dtype=jnp.float32) * sc_d
        Sd = jax.random.normal(ks[8], (F, D), dtype=jnp.float32) * sc_f
        return {'hidden_states': hidden_states, 'gating_probs': gating_probs, 'shared_gate_prob': shared_gate_prob, 'Wg': Wg, 'Wu': Wu, 'Wd': Wd, 'Sg': Sg, 'Su': Su, 'Sd': Sd}
    _L0_cond_all = _L0_cond_setup()
    _L0_cond_in = {k: v for k, v in _L0_cond_all.items() if k in ('Wg', 'Wu', 'Wd', 'Sg', 'Su', 'Sd')}
    del _L0_cond_all

    def _L1_cond_setup():
        import jax, jax.numpy as jnp
        import numpy as np
        NEG_INF = -1e+30
        key = jax.random.key(seed)
        k1, k2, k3, k4, k5 = jax.random.split(key, 5)
        B, S, D, A = (16, 256, 256, 64)
        hidden = jax.random.normal(k1, (B, S, D), dtype=jnp.float32)
        W1 = jax.random.normal(k2, (D, A), dtype=jnp.float32) / np.sqrt(D)
        b1 = jax.random.normal(k3, (A,), dtype=jnp.float32) * 0.01
        v = jax.random.normal(k4, (A,), dtype=jnp.float32) / np.sqrt(A)
        prompt_type_ids = jax.random.randint(k5, (B,), 0, 3, dtype=jnp.int32)
        return {'hidden': hidden, 'W1': W1, 'b1': b1, 'v': v, 'prompt_type_ids': prompt_type_ids}
    _L1_cond_all = _L1_cond_setup()
    _L1_cond_in = {k: v for k, v in _L1_cond_all.items() if k in ('W1', 'b1', 'v')}
    del _L1_cond_all
    return {'x': x, 'fside_Bx8_0': fside_Bx8_0, 'condB_sharedgateprob': condB_sharedgateprob, 'itok_B_0_2': itok_B_0_2, 'L0_cond_Wg': _L0_cond_in['Wg'], 'L0_cond_Wu': _L0_cond_in['Wu'], 'L0_cond_Wd': _L0_cond_in['Wd'], 'L0_cond_Sg': _L0_cond_in['Sg'], 'L0_cond_Su': _L0_cond_in['Su'], 'L0_cond_Sd': _L0_cond_in['Sd'], 'L1_cond_W1': _L1_cond_in['W1'], 'L1_cond_b1': _L1_cond_in['b1'], 'L1_cond_v': _L1_cond_in['v']}

def reference(x, fside_Bx8_0, condB_sharedgateprob, itok_B_0_2, L0_cond_Wg, L0_cond_Wu, L0_cond_Wd, L0_cond_Sg, L0_cond_Su, L0_cond_Sd, L1_cond_W1, L1_cond_b1, L1_cond_v):
    import jax
    import jax.numpy as jnp

    def _L0_cond_ref(hidden_states, gating_probs, shared_gate_prob, Wg, Wu, Wd, Sg, Su, Sd):
        import jax, jax.numpy as jnp
        import numpy as np
        E, B, S, D, F = (8, 2, 256, 256, 1024)
        h = hidden_states
        g = jnp.einsum('bsd,edf->ebsf', h, Wg)
        u = jnp.einsum('bsd,edf->ebsf', h, Wu)
        expert_outs = jnp.einsum('ebsf,efd->ebsd', jax.nn.silu(g) * u, Wd)
        expert_output = jnp.einsum('be,ebsd->bsd', gating_probs, expert_outs)
        shared = jnp.einsum('bsf,fd->bsd', jax.nn.silu(h @ Sg) * (h @ Su), Sd)
        sg = shared_gate_prob[:, :, None]
        return (1.0 - sg) * expert_output + sg * shared

    def _L1_cond_ref(hidden, W1, b1, v, prompt_type_ids):
        import jax, jax.numpy as jnp
        import numpy as np
        NEG_INF = -1e+30
        B, S, D = hidden.shape
        attn_in = jnp.tanh(jnp.einsum('bsd,da->bsa', hidden, W1) + b1)
        scores = jnp.einsum('bsa,a->bs', attn_in, v)
        idx = jnp.arange(S)
        j = idx[:, None]
        l = idx[None, :]
        prefix_m = l <= j
        postfix_m = l >= j
        cloze_m = l != j
        pt = prompt_type_ids[:, None, None]
        mask = jnp.where(pt == 0, prefix_m[None], jnp.where(pt == 1, postfix_m[None], cloze_m[None]))
        masked_scores = jnp.where(mask, scores[:, None, :], NEG_INF)
        p = jax.nn.softmax(masked_scores, axis=-1)
        cnt = jnp.sum(mask, axis=-1).astype(hidden.dtype)
        pooled = jnp.einsum('bjl,bld->bjd', p, hidden) / cnt[..., None]
        return pooled
    x = x + _L0_cond_ref(x, fside_Bx8_0, condB_sharedgateprob[:, None], L0_cond_Wg, L0_cond_Wu, L0_cond_Wd, L0_cond_Sg, L0_cond_Su, L0_cond_Sd)
    x = x + _L1_cond_ref(x, L1_cond_W1, L1_cond_b1, L1_cond_v, itok_B_0_2)
    return x

_drawn_inputs = setup_inputs


def setup_inputs(seed=0):
    import zlib

    import numpy as np

    out = dict(_drawn_inputs(seed))
    spreads = {}
    factors = {'L1_cond_W1': 19.605, 'L1_cond_b1': 64.0, 'L1_cond_v': 38.561}
    for name, (base, spread) in spreads.items():
        noise = np.random.default_rng([zlib.crc32(name.encode()), seed]).standard_normal(out[name].shape)
        drawn = base * np.exp(spread * noise) if base else spread * noise
        out[name] = jnp.asarray(drawn.astype(out[name].dtype))
    for name, factor in factors.items():
        out[name] = (out[name] * factor).astype(out[name].dtype)
    return out
```

```python
from contextlib import ExitStack

import concourse.bass as bass
from concourse import mybir

F32 = mybir.dt.float32
F32R = mybir.dt.float32r
I32 = mybir.dt.int32
ALU = mybir.AluOpType
ACT = mybir.ActivationFunctionType
AX_X = mybir.AxisListType.X

P = 128
BANK = 512
NEG_INF = -1e30


def cond_resid_kernel(nc, x, fside, shared_gate, prompt_type, Wg, Wu, Wd, Sg, Su, Sd, W1, b1, v, out):
    B, S, D = x.shape
    E, _, F = Wg.shape
    A = W1.shape[1]
    KD = D // P
    NT = S // BANK
    NJ = S // P
    NEXP = E + 1
    TILES = 4
    STEPS = NEXP * F // (P * TILES)
    HALVES = F // (P * TILES)
    UNITS = TILES * NT
    UB = STEPS * UNITS
    SLOT = 2
    NSLOT = TILES // SLOT
    SW = SLOT * P
    HS = 4
    LAG = 2
    JB = BANK // D
    XA = D + 4

    x_dram = x.rearrange("b (h j p) d -> b h p j d", p=P, j=NJ // NT)
    out_dram = out.rearrange("b (h j p) d -> b h p j d", p=P, j=NJ // NT)

    with ExitStack() as ctx:
        def sb(name, shape, dt=F32):
            return ctx.enter_context(nc.sbuf_tensor(name, shape, dt))

        def bank(name):
            return ctx.enter_context(nc.psum_tensor(name, [P, BANK], F32))

        def sem(name):
            return ctx.enter_context(nc.semaphore(name))

        x_nat = sb("x_nat", [P, B, NJ, D])
        xT = sb("xT", [P, B, KD, S])
        xT_hi = sb("xT_hi", [P, B, KD, S], F32R)
        xT_lo = sb("xT_lo", [P, B, KD, S], F32R)
        raw_gu = sb("raw_gu", [P, NSLOT, 2 * KD, SW])
        raw_d = sb("raw_d", [P, NSLOT, SLOT, D])
        wgu_hi = sb("wgu_hi", [P, TILES, 2 * KD, P], F32R)
        wgu_lo = sb("wgu_lo", [P, TILES, 2 * KD, P], F32R)
        wd_hi = sb("wd_hi", [P, TILES, D], F32R)
        wd_lo = sb("wd_lo", [P, TILES, D], F32R)
        gate_silu = sb("gate_silu", [P, 2, BANK])
        h = sb("h", [P, 2, BANK])
        h_hi = sb("h_hi", [P, HS, BANK], F32R)
        h_lo = sb("h_lo", [P, HS, BANK], F32R)
        probs = sb("probs", [P, B, E])
        sg = sb("sg", [P, B])
        sg_rest = sb("sg_rest", [P, B])
        gates = sb("gates", [P, B, NEXP, HALVES])
        ptype_i = sb("ptype_i", [P, B], I32)
        ptype = sb("ptype", [P, B])
        is_pre = sb("is_pre", [P, B])
        is_post = sb("is_post", [P, B])
        w_before = sb("w_before", [P, B])
        w_after = sb("w_after", [P, B])
        w_self = sb("w_self", [P, B])
        f_before = sb("f_before", [P, B])
        f_after = sb("f_after", [P, B])
        f_self = sb("f_self", [P, B])
        W1_sb = sb("W1_sb", [P, KD, A])
        b1_sb = sb("b1_sb", [A, 1])
        v_sb = sb("v_sb", [A, 1])
        v_rep = sb("v_rep", [A, P])
        ones = sb("ones", [P, P])
        zero = sb("zero", [P, 1])
        ident = sb("ident", [P, P])
        before = sb("before", [P, P])
        after = sb("after", [P, P])
        eye = sb("eye", [P, NJ, NJ])
        pos_i = sb("pos_i", [P, NJ], I32)
        pos = sb("pos", [P, NJ])
        mask = sb("mask", [P, B, P])
        blk_mask = sb("blk_mask", [NJ, B, S])
        cnt_rest = sb("cnt_rest", [P, B])
        cnt_slope = sb("cnt_slope", [P, B])
        cnt = sb("cnt", [P, B, NJ])
        attnT = sb("attnT", [A, B, S])
        score = sb("score", [P, B, S])
        score_self = sb("score_self", [P, B, S])
        max_before = sb("max_before", [P, B, S])
        qmax = sb("qmax", [P, B, S])
        score_col = sb("score_col", [P, B, NJ])
        blk_max = sb("blk_max", [P, B, NJ])
        blk_max_diag = sb("blk_max_diag", [NJ, B, NJ])
        blk_max_col = sb("blk_max_col", [NJ, B])
        e_blk = sb("e_blk", [P, B, NJ])
        e_diag = sb("e_diag", [P, B, NJ, NJ])
        carry = sb("carry", [NJ, B, S])
        blk_before, blk_after = (qmax[0:NJ, i, :].rearrange("i (j p) -> i j p", p=P) for i in range(2))
        probT = score_self[:].rearrange("p b (j q) -> p b j q", q=P)
        x1 = sb("x1", [P, B, NJ, XA])
        blk_sum = sb("blk_sum", [NJ, B, D + 1])
        den = sb("den", [P, B, NJ])
        rden = sb("rden", [P, B, NJ])

        acc = [[bank(f"acc{d}{t}") for t in range(NT)] for d in range(KD)]
        gate_ps = [bank(f"gate{i}") for i in range(2)]
        up_ps = [bank(f"up{i}") for i in range(2)]

        x_loaded = [[sem(f"x_loaded{b}{t}") for t in range(NT)] for b in range(B)]
        gates_loaded = sem("gates_loaded")
        l1_loaded = sem("l1_loaded")
        ones_ready = sem("ones_ready")
        ident_ready = sem("ident_ready")
        const_step = sem("const_step")
        gate_step = sem("gate_step")
        xT_done = sem("xT_done")
        xT_copied = sem("xT_copied")
        x_hi_done = sem("x_hi_done")
        x_split0 = sem("x_split0")
        x_hi1_done = sem("x_hi1_done")
        x_split1 = sem("x_split1")
        staged = [sem(f"staged{s}") for s in range(NSLOT)]
        gu_hi_done = sem("gu_hi_done")
        gu_split = sem("gu_split")
        d_hi_done = sem("d_hi_done")
        d_split = sem("d_split")
        gate_done = sem("gate_done")
        up_done = sem("up_done")
        silu_done = sem("silu_done")
        h_done = sem("h_done")
        h_hi_done = sem("h_hi_done")
        h_split = sem("h_split")
        down_done = sem("down_done")
        x1T_done = sem("x1T_done")
        attn_done = sem("attn_done")
        tanh_done = sem("tanh_done")
        x1_done = sem("x1_done")
        x1_copied = sem("x1_copied")
        score_done = sem("score_done")
        score_copied = sem("score_copied")
        self_done = sem("self_done")
        col_done = sem("col_done")
        col_copied = sem("col_copied")
        dve_l1 = sem("dve_l1")
        e_done = sem("e_done")
        carry_arg = sem("carry_arg")
        carry_done = sem("carry_done")
        prob_done = sem("prob_done")
        sum_done = sem("sum_done")
        sum_copied = sem("sum_copied")
        den_done = sem("den_done")
        pool_done = sem("pool_done")
        out_done = sem("out_done")
        stored = sem("stored")

        DVE_L1 = {}
        for b in range(B):
            for s in ("before0", "before", "after0", "after", "max1", "qmax", "parg", "blkmax", "diag", "blkcol", "earg"):
                DVE_L1[s, b] = len(DVE_L1) + 1
        for b in range(B):
            for s in ("ediag", "den", "rden"):
                DVE_L1[s, b] = len(DVE_L1) + 1

        CONST_STEPS = 2 + 4 + 1 + 2 + 1 + 1 + 6 + 3 + 3 + B * (2 + 4 + 3 + 2)

        ATTN = [gate_ps[0], up_ps[0]]
        X1 = [gate_ps[1], up_ps[1]]
        SCORE = [[acc[b][t] for t in range(NT)] for b in range(B)]
        COL = [ATTN[b][:, 0:NJ] for b in range(B)]
        DEN = [ATTN[b][:, NJ:2 * NJ] for b in range(B)]
        SUM = [X1[b][0:NJ, 0:D + 1] for b in range(B)]
        POOLED = [acc[d][t] for d in range(KD) for t in range(NT)]

        block = ctx.enter_context(nc.Block())

        @block.sync
        def _(sp):
            def load_x(b, t):
                n = NJ // NT
                sp.dma_start(x_nat[:, b, t * n:(t + 1) * n, :], x_dram[b, t]).then_inc(x_loaded[b][t], 16)

            def load_slot(s, g, u, d, f0):
                for n, w in enumerate((g, u)):
                    sp.dma_start(raw_gu[:, s, n * KD:(n + 1) * KD, :],
                                 w[:, f0:f0 + SW].rearrange("(k p) f -> p k f", p=P)).then_inc(staged[s], 16)
                sp.dma_start(raw_d[:, s, :, :],
                             d[f0:f0 + SW, :].rearrange("(j p) d -> p j d", p=P)).then_inc(staged[s], 16)

            def load_expert(g, u, d, slot0, fresh=False):
                for n in range(HALVES * NSLOT):
                    if not (fresh and n < NSLOT):
                        sp.wait_ge(d_split, (slot0 + n - NSLOT + 1) * SLOT)
                    load_slot(n % NSLOT, g, u, d, n * SW)

            per = HALVES * NSLOT
            load_x(0, 0)
            load_slot(0, Wg[0], Wu[0], Wd[0], 0)
            load_x(0, 1)
            load_slot(1, Wg[0], Wu[0], Wd[0], SW)
            for t in range(NT):
                load_x(1, t)
            for n in range(NSLOT, per):
                sp.wait_ge(d_split, (n - NSLOT + 1) * SLOT)
                load_slot(n % NSLOT, Wg[0], Wu[0], Wd[0], n * SW)
            with sp.Fori(1, E) as e:
                load_expert(Wg[e], Wu[e], Wd[e], e * per)
            load_expert(Sg, Su, Sd, E * per)
            with sp.Fori(0, E) as e:
                load_expert(Wg[e], Wu[e], Wd[e], e * per + NEXP * per)
            load_expert(Sg, Su, Sd, (NEXP + E) * per)

            for b in range(B):
                for t in range(NT):
                    n = NJ // NT
                    sp.wait_ge(out_done, b * NJ + (t + 1) * n)
                    sp.dma_start(out_dram[b, t], x_nat[:, b, t * n:(t + 1) * n, :]).then_inc(stored, 16)
            sp.wait_ge(stored, 16 * B * NT)

        @block.gpsimd
        def _(pool):
            steps = [0]

            def const(ins):
                steps[0] += 1
                ins.then_inc(const_step, 1)
                pool.wait_ge(const_step, steps[0])

            nc.gpsimd.memset(zero[:], 0.0).then_inc(ones_ready, 1)
            nc.gpsimd.memset(ones[:], 1.0).then_inc(ones_ready, 1)
            pool.wait_ge(ones_ready, 2)
            nc.gpsimd.affine_select(out=ident[:], in_=ones[:], compare_op=ALU.is_equal, fill=0.0, base=0,
                                    pattern=[[1, P]], channel_multiplier=-1).then_inc(ident_ready, 1)

            def split_tile(f, step, first=False):
                s, j = f // SLOT, f % SLOT
                n = step * TILES + f
                if j == 0:
                    pool.wait_ge(staged[s], (step + 1) * 3 * 16)
                gu = raw_gu[:, s, :, j * P:(j + 1) * P]
                if not first:
                    pool.wait_ge(up_done, (n - TILES + 1) * NT)
                nc.gpsimd.tensor_tensor(wgu_hi[:, f, :, :], gu,
                                        zero[:, 0:1].unsqueeze(2).broadcast_to([P, 2 * KD, P]), ALU.add).then_inc(gu_hi_done, 1)
                pool.wait_ge(gu_hi_done, n + 1)
                nc.gpsimd.tensor_tensor(wgu_lo[:, f, :, :], gu, wgu_hi[:, f, :, :].bitcast(F32),
                                        ALU.subtract).then_inc(gu_split, 1)
                if not first:
                    pool.wait_ge(down_done, (n - TILES + 1) * NT)
                nc.gpsimd.tensor_tensor(wd_hi[:, f, :], raw_d[:, s, j, :], zero[:, 0:1].broadcast_to([P, D]),
                                        ALU.add).then_inc(d_hi_done, 1)
                pool.wait_ge(d_hi_done, n + 1)
                nc.gpsimd.tensor_tensor(wd_lo[:, f, :], raw_d[:, s, j, :], wd_hi[:, f, :].bitcast(F32),
                                        ALU.subtract).then_inc(d_split, 1)

            for f in range(TILES):
                split_tile(f, 0, first=True)

            pool.wait_ge(xT_copied, 2 * KD * NT)
            for k in range(KD):
                for t in range(NT):
                    half = slice(t * BANK, (t + 1) * BANK)
                    nc.gpsimd.tensor_copy(xT_hi[:, 1, k, half], xT[:, 1, k, half]).then_inc(x_hi1_done, 1)
                    pool.wait_ge(x_hi1_done, k * NT + t + 1)
                    nc.gpsimd.tensor_tensor(xT_lo[:, 1, k, half], xT[:, 1, k, half],
                                            xT_hi[:, 1, k, half].bitcast(F32), ALU.subtract).then_inc(x_split1, 1)

            with pool.Fori(1, 2) as step:
                for f in range(TILES):
                    split_tile(f, step)

            for m, sign in ((before, 1), (after, -1)):
                nc.gpsimd.affine_select(out=m[:], in_=ones[:], compare_op=ALU.is_gt, fill=0.0, base=0,
                                        pattern=[[sign, P]], channel_multiplier=-sign).then_inc(const_step, 1)
                steps[0] += 1
            for m, sign in ((blk_before, 1), (blk_after, -1)):
                const(nc.gpsimd.memset(m, 1.0))
                const(nc.gpsimd.affine_select(out=m, in_=m, compare_op=ALU.is_gt, fill=0.0, base=0,
                                              pattern=[[sign, NJ], [0, P]], channel_multiplier=-sign))
            const(nc.gpsimd.affine_select(out=eye[:], in_=ones[:, 0:NJ * NJ].rearrange("p (i j) -> p i j", j=NJ),
                                          compare_op=ALU.is_equal, fill=0.0, base=0,
                                          pattern=[[1, NJ], [-1, NJ]], channel_multiplier=0))
            const(nc.gpsimd.iota(pos_i[:], pattern=[[P, NJ]], base=0, channel_multiplier=1))
            const(nc.gpsimd.tensor_copy(pos[:], pos_i[:]))
            const(nc.gpsimd.memset(x1[:, :, :, D:XA], 1.0))
            pool.wait_ge(l1_loaded, 4 * 16)
            const(nc.gpsimd.tensor_scalar(v_rep[:], ones[0:A, :], v_sb[:, 0:1], None, ALU.mult))
            const(nc.gpsimd.tensor_copy(ptype[:], ptype_i[:]))
            const(nc.gpsimd.tensor_scalar(is_pre[:], ptype[:], 0.0, None, ALU.is_equal))
            const(nc.gpsimd.tensor_scalar(is_post[:], ptype[:], 1.0, None, ALU.is_equal))
            const(nc.gpsimd.tensor_scalar(w_before[:], is_post[:], -1.0, 1.0, ALU.mult, ALU.add))
            const(nc.gpsimd.tensor_scalar(w_after[:], is_pre[:], -1.0, 1.0, ALU.mult, ALU.add))
            const(nc.gpsimd.tensor_tensor(w_self[:], is_pre[:], is_post[:], ALU.add))
            for flag, w in ((f_before, w_before), (f_after, w_after), (f_self, w_self)):
                const(nc.gpsimd.tensor_scalar(flag[:], w[:], 1.0, -NEG_INF, ALU.subtract, ALU.mult))
            const(nc.gpsimd.tensor_tensor(cnt_slope[:], w_before[:], w_after[:], ALU.subtract))
            const(nc.gpsimd.tensor_scalar(cnt_rest[:], w_after[:], float(S - 1), None, ALU.mult))
            const(nc.gpsimd.tensor_tensor(cnt_rest[:], cnt_rest[:], w_self[:], ALU.add))
            for b in range(B):
                one = slice(b, b + 1)
                const(nc.gpsimd.tensor_scalar(cnt[:, b, :], pos[:], cnt_slope[:, one], cnt_rest[:, one],
                                              ALU.mult, ALU.add))
                const(nc.gpsimd.tensor_scalar(mask[:, b, :], ident[:], w_self[:, one], None, ALU.mult))
                for m, w in ((before, w_before), (after, w_after)):
                    const(nc.gpsimd.tensor_scalar(probT[:, b, 0, :], m[:], w[:, one], None, ALU.mult))
                    const(nc.gpsimd.tensor_tensor(mask[:, b, :], mask[:, b, :], probT[:, b, 0, :], ALU.add))
                const(nc.gpsimd.tensor_scalar(blk_mask[:, b], blk_before.rearrange("i j p -> i (j p)"), w_before[0:NJ, one], None, ALU.mult))
                const(nc.gpsimd.tensor_scalar(carry[:, b], blk_after.rearrange("i j p -> i (j p)"),
                                              w_after[0:NJ, one], None, ALU.mult))
                const(nc.gpsimd.tensor_tensor(blk_mask[:, b], blk_mask[:, b], carry[:, b], ALU.add))
                for m in (mask[:, b], blk_mask[:, b]):
                    const(nc.gpsimd.tensor_scalar(m, m, 1.0, -NEG_INF, ALU.subtract, ALU.mult))
            assert steps[0] == CONST_STEPS

            with pool.Fori(2, B * STEPS) as step:
                for f in range(TILES):
                    split_tile(f, step)

            for b in range(B):
                pool.wait_ge(score_copied, NT * (b + 1))
                nc.gpsimd.tensor_scalar(score_self[:, b, :], score[:, b, :], f_self[:, b:b + 1], None,
                                        ALU.add).then_inc(self_done, 1)
            for b in range(B):
                pool.wait_ge(dve_l1, DVE_L1["qmax", b])
                nc.gpsimd.tensor_tensor(carry[:, b], blk_mask[:, b], qmax[0:NJ, b, :],
                                        ALU.subtract).then_inc(carry_arg, 1)

        @block.scalar
        def _(act):
            act.dma_start(probs[:], fside.unsqueeze(0).broadcast_to([P, B, E])).then_inc(gates_loaded, 16)
            act.dma_start(sg[:], shared_gate.unsqueeze(0).broadcast_to([P, B])).then_inc(gates_loaded, 16)
            act.dma_start(ptype_i[:], prompt_type.unsqueeze(0).broadcast_to([P, B])).then_inc(l1_loaded, 16)
            act.dma_start(W1_sb[:], W1.rearrange("(k p) a -> p k a", p=P)).then_inc(l1_loaded, 16)
            act.dma_start(b1_sb[:], b1.unsqueeze(1)).then_inc(l1_loaded, 16)
            act.dma_start(v_sb[:], v.unsqueeze(1)).then_inc(l1_loaded, 16)

            for b in range(B):
                for t in range(NT):
                    for k in range(KD):
                        act.wait_ge(xT_done, (b * NT + t) * KD + k + 1)
                        nc.scalar.activation(xT[:, b, k, t * BANK:(t + 1) * BANK], acc[k][t][:],
                                             ACT.Copy).then_inc(xT_copied, 1)

            with act.Fori(0, B * STEPS) as step:
                for u in range(UNITS):
                    act.wait_ge(gate_done, step * UNITS + (u + 1))
                    nc.scalar.activation(gate_silu[:, u % 2, :], gate_ps[u % 2][:], ACT.Silu).then_inc(silu_done, 1)

            def tanh(b):
                for t in range(NT):
                    act.wait_ge(attn_done, b * NT + t + 1)
                    nc.scalar.activation(attnT[:, b, t * BANK:(t + 1) * BANK], ATTN[t][0:A, :], ACT.Tanh,
                                         bias=b1_sb[:, 0:1]).then_inc(tanh_done, 1)

            def copy_x1(b):
                for n in range(NJ // JB):
                    act.wait_ge(x1_done, b * (NJ // JB) + n + 1)
                    nc.scalar.activation(x1[:, b, n * JB:(n + 1) * JB, 0:D],
                                         X1[n % 2][:].rearrange("p (j d) -> p j d", d=D),
                                         ACT.Copy).then_inc(x1_copied, 1)

            def copy_score(b):
                for t in range(NT):
                    act.wait_ge(score_done, b * NT + t + 1)
                    nc.scalar.activation(score[:, b, t * BANK:(t + 1) * BANK], SCORE[b][t][:],
                                         ACT.Copy).then_inc(score_copied, 1)

            def copy_col(b):
                act.wait_ge(col_done, b + 1)
                nc.scalar.activation(score_col[:, b, :], COL[b], ACT.Copy).then_inc(col_copied, 1)

            def exps(b):
                act.wait_ge(dve_l1, DVE_L1["earg", b])
                nc.scalar.activation(e_blk[:, b, :], e_blk[:, b, :], ACT.Exp).then_inc(e_done, 1)
                act.wait_ge(carry_arg, b + 1)
                nc.scalar.activation(carry[:, b, :], carry[:, b, :], ACT.Exp,
                                     bias=blk_max_col[:, b:b + 1]).then_inc(carry_done, 1)
                act.wait_ge(dve_l1, DVE_L1["parg", b])
                act.wait_ge(col_copied, b + 1)
                for j in range(NJ):
                    nc.scalar.activation(probT[:, b, j, :], probT[:, b, j, :], ACT.Exp,
                                         bias=score_col[:, b, j:j + 1]).then_inc(prob_done, 1)

            def copy_sum(b):
                act.wait_ge(sum_done, b + 1)
                nc.scalar.activation(blk_sum[:, b, :], SUM[b], ACT.Copy).then_inc(sum_copied, 1)

            tanh(0)
            copy_x1(0)
            tanh(1)
            copy_score(0)
            copy_x1(1)
            copy_score(1)
            copy_col(0)
            copy_col(1)
            exps(0)
            copy_sum(0)
            exps(1)
            copy_sum(1)

        @block.vector
        def _(dve):
            dve.wait_ge(gates_loaded, 2 * 16)
            nc.vector.tensor_scalar(sg_rest[:], sg[:], -1.0, 1.0, ALU.mult, ALU.add).then_inc(gate_step, 1)
            dve.wait_ge(gate_step, 1)
            for b in range(B):
                for n in range(HALVES):
                    nc.vector.tensor_scalar(gates[:, b, 0:E, n], probs[:, b, :], sg_rest[:, b:b + 1], None,
                                            ALU.mult).then_inc(gate_step, 1)
                    nc.vector.tensor_copy(gates[:, b, E:NEXP, n], sg[:, b:b + 1]).then_inc(gate_step, 1)
            gate_of = gates[:].rearrange("p b e n -> p (b e n)")

            for t in range(NT):
                for k in range(KD):
                    n = t * KD + k + 1
                    half = slice(t * BANK, (t + 1) * BANK)
                    dve.wait_ge(xT_copied, n)
                    nc.vector.tensor_copy(xT_hi[:, 0, k, half], xT[:, 0, k, half]).then_inc(x_hi_done, 1)
                    dve.wait_ge(x_hi_done, n)
                    nc.vector.tensor_tensor(xT_lo[:, 0, k, half], xT[:, 0, k, half],
                                            xT_hi[:, 0, k, half].bitcast(F32), ALU.subtract).then_inc(x_split0, 1)
            dve.wait_ge(gate_step, 1 + 2 * B * HALVES)

            for b in range(B):
                with dve.Fori(b * STEPS, (b + 1) * STEPS) as step:
                    for u in range(UNITS):
                        n = step * UNITS + (u + 1)
                        i, s = u % 2, u % HS
                        dve.wait_ge(silu_done, n)
                        dve.wait_ge(up_done, n)
                        nc.vector.scalar_tensor_tensor(out=h[:, i, :], in0=gate_silu[:, i, :],
                                                       scalar=gate_of[:, bass.ds(step, 1)], in1=up_ps[i][:],
                                                       op0=ALU.mult, op1=ALU.mult).then_inc(h_done, 1)
                        dve.wait_ge(h_done, n)
                        nc.vector.tensor_copy(h_hi[:, s, :], h[:, i, :]).then_inc(h_hi_done, 1)
                        dve.wait_ge(h_hi_done, n)
                        nc.vector.tensor_tensor(h_lo[:, s, :], h[:, i, :], h_hi[:, s, :].bitcast(F32),
                                                ALU.subtract).then_inc(h_split, 1)
                dve.wait_ge(down_done, (b + 1) * UB)
                for t in range(NT):
                    for k in range(KD):
                        half = slice(t * BANK, (t + 1) * BANK)
                        nc.vector.tensor_tensor(xT[:, b, k, half], acc[k][t][:], xT[:, b, k, half],
                                                ALU.add).then_inc(x1T_done, 1)

            def step_done(name, b, ins):
                ins.then_inc(dve_l1, 1)
                return DVE_L1[name, b]

            def after_step(name, b):
                dve.wait_ge(dve_l1, DVE_L1[name, b])

            def maxima(b):
                one = slice(b, b + 1)
                sc = score[:, b, :]
                step_done("before0", b, nc.vector.memset(max_before[:, b, 0:1], NEG_INF))
                dve.wait_ge(score_copied, NT * (b + 1))
                step_done("before", b, nc.vector.tensor_tensor_scan(
                    max_before[:, b, 1:S], sc[:, 0:S - 1], sc[:, 0:S - 1], NEG_INF, ALU.max, ALU.max))
                step_done("after0", b, nc.vector.memset(qmax[:, b, S - 1:S], NEG_INF))
                step_done("after", b, nc.vector.tensor_tensor_scan(
                    qmax[:, b, S - 2::-1], sc[:, S - 1:0:-1], sc[:, S - 1:0:-1], NEG_INF, ALU.max, ALU.max))
                after_step("before", b)
                dve.wait_ge(self_done, b + 1)
                dve.wait_ge(const_step, CONST_STEPS)
                step_done("max1", b, nc.vector.scalar_tensor_tensor(
                    out=score_self[:, b, :], in0=max_before[:, b, :], scalar=f_before[:, one],
                    in1=score_self[:, b, :], op0=ALU.add, op1=ALU.max))
                after_step("max1", b)
                step_done("qmax", b, nc.vector.scalar_tensor_tensor(
                    out=qmax[:, b, :], in0=qmax[:, b, :], scalar=f_after[:, one],
                    in1=score_self[:, b, :], op0=ALU.add, op1=ALU.max))
                after_step("qmax", b)
                step_done("parg", b, nc.vector.tensor_tensor(
                    probT[:, b], mask[:, b, :].unsqueeze(1).broadcast_to([P, NJ, P]),
                    qmax[:, b, :].rearrange("p (j q) -> p j q", q=P), ALU.subtract))
                step_done("blkmax", b, nc.vector.tensor_reduce(
                    blk_max[:, b, :], sc.rearrange("p (j l) -> p j l", l=P), AX_X, ALU.max))
                after_step("blkmax", b)
                step_done("diag", b, nc.vector.tensor_tensor(
                    blk_max_diag[:, b, :], blk_max[0:NJ, b, :], ident[0:NJ, 0:NJ], ALU.mult))
                after_step("diag", b)
                step_done("blkcol", b, nc.vector.tensor_reduce(
                    blk_max_col[:, one], blk_max_diag[:, b, :], AX_X, ALU.add))
                dve.wait_ge(col_copied, b + 1)
                step_done("earg", b, nc.vector.tensor_tensor(
                    e_blk[:, b, :], score_col[:, b, :], blk_max[:, b, :], ALU.subtract))

            def weights(b):
                dve.wait_ge(e_done, b + 1)
                step_done("ediag", b, nc.vector.tensor_tensor(
                    e_diag[:, b], e_blk[:, b, :].unsqueeze(2).broadcast_to([P, NJ, NJ]), eye[:], ALU.mult))

            def finish(b):
                dve.wait_ge(den_done, b + 1)
                step_done("den", b, nc.vector.tensor_tensor(den[:, b, :], DEN[b], cnt[:, b, :], ALU.mult))
                after_step("den", b)
                step_done("rden", b, nc.vector.reciprocal(rden[:, b, :], den[:, b, :]))
                after_step("rden", b)
                for j in range(NJ):
                    dve.wait_ge(pool_done, b * NJ // JB + j // JB + 1)
                    nc.vector.scalar_tensor_tensor(
                        out=x_nat[:, b, j, :], in0=POOLED[j // JB][:, j % JB * D:(j % JB + 1) * D],
                        scalar=rden[:, b, j:j + 1], in1=x1[:, b, j, 0:D], op0=ALU.mult,
                        op1=ALU.add).then_inc(out_done, 1)

            maxima(0)
            maxima(1)
            weights(0)
            finish(0)
            weights(1)
            finish(1)

        @block.tensor
        def _(pe):
            def transpose_x(b):
                n = NJ // NT
                for t in range(NT):
                    pe.wait_ge(x_loaded[b][t], 16)
                    for k in range(KD):
                        if b:
                            pe.wait_ge(xT_copied, ((b - 1) * NT + t) * KD + k + 1)
                        for j in range(n):
                            last = nc.tensor.transpose(acc[k][t][:, j * P:(j + 1) * P],
                                                       x_nat[:, b, t * n + j, k * P:(k + 1) * P], ident[:])
                        last.then_inc(xT_done, 1)

            def three_pass(ps, w_hi, w_lo, a_hi, a_lo, start, stop):
                nc.tensor.matmul(ps, w_hi, a_hi, start=start, stop=False)
                nc.tensor.matmul(ps, w_hi, a_lo, start=False, stop=False)
                return nc.tensor.matmul(ps, w_lo, a_hi, start=False, stop=stop)

            def gate_up(b, u, step):
                f, t = u // NT, u % NT
                half = slice(t * BANK, (t + 1) * BANK)
                if t == 0:
                    pe.wait_ge(gu_split, step * TILES + (f + 1))
                if not (isinstance(step, int) and step * UNITS + u < 2):
                    pe.wait_ge(h_done, step * UNITS + (u - 1))
                for ps, w0, done in ((gate_ps[u % 2], 0, gate_done), (up_ps[u % 2], KD, up_done)):
                    for k in range(KD):
                        last = three_pass(ps[:], wgu_hi[:, f, w0 + k, :], wgu_lo[:, f, w0 + k, :],
                                          xT_hi[:, b, k, half], xT_lo[:, b, k, half], k == 0, k == KD - 1)
                    last.then_inc(done, 1)

            def down(u, step, start=False, stop=False):
                f, t = u // NT, u % NT
                if t == 0:
                    pe.wait_ge(d_split, step * TILES + (f + 1))
                pe.wait_ge(h_split, step * UNITS + (u + 1))
                for d in range(KD):
                    cols = slice(d * P, (d + 1) * P)
                    last = three_pass(acc[d][t][:], wd_hi[:, f, cols], wd_lo[:, f, cols],
                                      h_hi[:, u % HS, :], h_lo[:, u % HS, :], start, stop)
                last.then_inc(down_done, 1)

            pe.wait_ge(ident_ready, 1)
            transpose_x(0)
            for b in range(B):
                s0 = b * STEPS
                if b == 0:
                    pe.wait_ge(x_split0, KD)
                    gate_up(0, 0, 0)
                    transpose_x(1)
                    pe.wait_ge(x_split0, KD * NT)
                    gate_up(0, 1, 0)
                    pe.wait_ge(xT_copied, B * KD * NT)
                gate_up(b, 2, s0)
                if b:
                    pe.wait_ge(x1T_done, b * KD * NT)
                down(0, s0, start=True)
                gate_up(b, 3, s0)
                down(1, s0, start=True)
                with pe.Fori(s0, s0 + STEPS - 1) as step:
                    for u in range(LAG + 2, UNITS):
                        gate_up(b, u, step)
                        down(u - LAG, step)
                    for u in range(LAG):
                        gate_up(b, u, step + 1)
                        down(UNITS - LAG + u, step)
                    for u in range(LAG, LAG + 2):
                        gate_up(b, u, step + 1)
                        down(u - LAG, step + 1)
                last = s0 + STEPS - 1
                for u in range(LAG + 2, UNITS):
                    gate_up(b, u, last)
                    down(u - LAG, last)
                if b + 1 < B:
                    pe.wait_ge(x_split1, KD * NT)
                    for u in range(LAG):
                        gate_up(b + 1, u, last + 1)
                        down(UNITS - LAG + u, last, stop=True)

            def attn(b):
                for t in range(NT):
                    if b:
                        pe.wait_ge(tanh_done, (b - 1) * NT + t + 1)
                    for k in range(KD):
                        mm = nc.tensor.matmul(ATTN[t][0:A, :], W1_sb[:, k, :],
                                              xT[:, b, k, t * BANK:(t + 1) * BANK], start=k == 0, stop=k == KD - 1)
                    mm.then_inc(attn_done, 1)

            def transpose_x1(b):
                for n in range(NJ // JB):
                    g = b * (NJ // JB) + n
                    if g >= 2:
                        pe.wait_ge(x1_copied, g - 1)
                    for j in range(JB):
                        for k in range(KD):
                            tok = (n * JB + j) * P
                            mm = nc.tensor.transpose(X1[n % 2][:, j * D + k * P:j * D + (k + 1) * P],
                                                     xT[:, b, k, tok:tok + P], ident[:])
                    mm.then_inc(x1_done, 1)

            def score_row(b):
                for t in range(NT):
                    pe.wait_ge(tanh_done, b * NT + t + 1)
                    nc.tensor.matmul(SCORE[b][t][:], v_rep[:], attnT[:, b, t * BANK:(t + 1) * BANK],
                                     start=True, stop=True).then_inc(score_done, 1)

            def score_cols(b):
                for j in range(NJ):
                    mm = nc.tensor.matmul(COL[b][:, j:j + 1], attnT[:, b, j * P:(j + 1) * P], v_sb[:, 0:1],
                                          start=True, stop=True)
                mm.then_inc(col_done, 1)

            def block_sums(b):
                pe.wait_ge(dve_l1, DVE_L1["ediag", b])
                pe.wait_ge(x1_copied, (NJ // JB) * (b + 1))
                for j in range(NJ):
                    mm = nc.tensor.matmul(SUM[b], e_diag[:, b, j, :], x1[:, b, j, 0:D + 1],
                                          start=j == 0, stop=j == NJ - 1)
                mm.then_inc(sum_done, 1)

            def pooled(b):
                pe.wait_ge(prob_done, NJ * (b + 1))
                pe.wait_ge(sum_copied, b + 1)
                pe.wait_ge(carry_done, b + 1)
                for j in range(NJ):
                    nc.tensor.matmul(DEN[b][:, j:j + 1], probT[:, b, j, :], x1[:, b, j, D:D + 1],
                                     start=True, stop=False)
                    mm = nc.tensor.matmul(DEN[b][:, j:j + 1], carry[:, b, j * P:(j + 1) * P], blk_sum[:, b, D:D + 1],
                                          start=False, stop=True)
                mm.then_inc(den_done, 1)
                for j in range(NJ):
                    if b and j % JB == 0:
                        pe.wait_ge(out_done, (b - 1) * NJ + j + JB)
                    ps = POOLED[j // JB][:, j % JB * D:(j % JB + 1) * D]
                    nc.tensor.matmul(ps, probT[:, b, j, :], x1[:, b, j, 0:D], start=True, stop=False)
                    mm = nc.tensor.matmul(ps, carry[:, b, j * P:(j + 1) * P], blk_sum[:, b, 0:D],
                                          start=False, stop=True)
                    if j % JB == JB - 1:
                        mm.then_inc(pool_done, 1)

            pe.wait_ge(const_step, CONST_STEPS)
            pe.wait_ge(h_done, B * UB - 1)
            attn(0)
            for u in range(UNITS - LAG, UNITS):
                down(u, B * STEPS - 1, stop=True)
            transpose_x1(0)
            pe.wait_ge(x1T_done, B * KD * NT)
            attn(1)
            score_row(0)
            transpose_x1(1)
            score_row(1)
            score_cols(0)
            score_cols(1)
            pe.wait_ge(score_copied, B * NT)
            block_sums(0)
            pooled(0)
            block_sums(1)
            pooled(1)


_INS = ["x", "fside_Bx8_0", "condB_sharedgateprob", "itok_B_0_2", "L0_cond_Wg", "L0_cond_Wu", "L0_cond_Wd",
        "L0_cond_Sg", "L0_cond_Su", "L0_cond_Sd", "L1_cond_W1", "L1_cond_b1", "L1_cond_v"]


def kernel(**inputs):
    import numpy as np
    import concourse.bacc as bacc
    from concourse.bass_utils import run_bass_kernel_spmd

    nc = bacc.Bacc("TRN2", target_bir_lowering=False, num_devices=1)
    arrays, args = {}, []
    for name in _INS:
        a = np.ascontiguousarray(inputs[name])
        arrays[f"in_{name}"] = a
        args.append(nc.dram_tensor(f"in_{name}", a.shape, mybir.dt.from_np(a.dtype), kind="ExternalInput").ap())
    args.append(nc.dram_tensor("out_x", inputs["x"].shape, F32, kind="ExternalOutput").ap())
    cond_resid_kernel(nc, *args)
    return run_bass_kernel_spmd(nc, [arrays], core_ids=[0]).results[0]["out_x"]
```

```python
from contextlib import ExitStack

import concourse.bass as bass
from concourse import mybir

F32 = mybir.dt.float32
F32R = mybir.dt.float32r
I32 = mybir.dt.int32
ALU = mybir.AluOpType
ACT = mybir.ActivationFunctionType
AX_X = mybir.AxisListType.X

P = 128
BANK = 512
NEG_INF = -1e30


def cond_resid_kernel(nc, x, fside, shared_gate, prompt_type, Wg, Wu, Wd, Sg, Su, Sd, W1, b1, v, out):
    B, S, D = x.shape
    E, _, F = Wg.shape
    A = W1.shape[1]
    KD = D // P
    NT = S // BANK
    NJ = S // P
    NEXP = E + 1
    TILES = 4
    STEPS = NEXP * F // (P * TILES)
    HALVES = F // (P * TILES)
    UNITS = TILES * NT
    UB = STEPS * UNITS
    SLOT = 2
    NSLOT = TILES // SLOT
    SW = SLOT * P
    LAG = 2
    HS = LAG
    LAST = UNITS + UNITS // 2
    JB = BANK // D
    NB = NJ // JB
    XA = D + 4

    x_dram = x.rearrange("b (h j p) d -> b h p j d", p=P, j=NJ // NT)
    out_dram = out.rearrange("b (h j p) d -> b h p j d", p=P, j=NJ // NT)

    with ExitStack() as ctx:
        def sb(name, shape, dt=F32):
            return ctx.enter_context(nc.sbuf_tensor(name, shape, dt))

        def bank(name):
            return ctx.enter_context(nc.psum_tensor(name, [P, BANK], F32))

        def sem(name):
            return ctx.enter_context(nc.semaphore(name))

        x_nat = sb("x_nat", [P, B, NJ, D])
        xT = sb("xT", [P, B, KD, S])
        xT_hi = sb("xT_hi", [P, B, KD, S], F32R)
        xT_lo = sb("xT_lo", [P, B, KD, S], F32R)
        raw_gu = sb("raw_gu", [P, NSLOT, 2 * KD, SW])
        raw_d = sb("raw_d", [P, NSLOT, SLOT, D])
        wgu_hi = sb("wgu_hi", [P, TILES, 2 * KD, P], F32R)
        wgu_lo = sb("wgu_lo", [P, TILES, 2 * KD, P], F32R)
        wd_hi = sb("wd_hi", [P, TILES, D], F32R)
        wd_lo = sb("wd_lo", [P, TILES, D], F32R)
        gate_silu = sb("gate_silu", [P, 2, BANK])
        h = sb("h", [P, 2, BANK])
        h_hi = sb("h_hi", [P, HS, BANK], F32R)
        h_lo = sb("h_lo", [P, HS, BANK], F32R)
        probs = sb("probs", [P, B, E])
        sg = sb("sg", [P, B])
        sg_rest = sb("sg_rest", [P, B])
        gates = sb("gates", [P, B, NEXP, HALVES])
        ptype_i = sb("ptype_i", [P, B], I32)
        ptype = sb("ptype", [P, B])
        is_pre = sb("is_pre", [P, B])
        is_post = sb("is_post", [P, B])
        w_before = sb("w_before", [P, B])
        w_after = sb("w_after", [P, B])
        w_self = sb("w_self", [P, B])
        f_before = sb("f_before", [P, B])
        f_after = sb("f_after", [P, B])
        f_self = sb("f_self", [P, B])
        W1_sb = sb("W1_sb", [P, KD, A])
        b1_sb = sb("b1_sb", [A, 1])
        v_sb = sb("v_sb", [A, 1])
        v_rep = sb("v_rep", [A, P])
        ones = sb("ones", [P, P])
        zero = sb("zero", [P, 1])
        ident = sb("ident", [P, P])
        before = sb("before", [P, P])
        after = sb("after", [P, P])
        eye = sb("eye", [P, NJ, NJ])
        pos_i = sb("pos_i", [P, NJ], I32)
        pos = sb("pos", [P, NJ])
        mask = sb("mask", [P, B, P])
        blk_mask = sb("blk_mask", [NJ, B, S])
        cnt_rest = sb("cnt_rest", [P, B])
        cnt_slope = sb("cnt_slope", [P, B])
        cnt = sb("cnt", [P, B, NJ])
        attnT = sb("attnT", [A, B, S])
        score = sb("score", [P, B, S])
        score_self = sb("score_self", [P, B, S])
        max_before = sb("max_before", [P, B, S])
        qmax = sb("qmax", [P, B, S])
        score_col = sb("score_col", [P, B, NJ])
        blk_max = sb("blk_max", [P, B, NJ])
        blk_max_diag = sb("blk_max_diag", [NJ, B, NJ])
        blk_max_col = sb("blk_max_col", [NJ, B])
        e_blk = sb("e_blk", [P, B, NJ])
        e_diag = sb("e_diag", [P, B, NJ, NJ])
        carry = sb("carry", [NJ, B, S])
        blk_before, blk_after = (qmax[0:NJ, i, :].rearrange("i (j p) -> i j p", p=P) for i in range(2))
        probT = score_self[:].rearrange("p b (j q) -> p b j q", q=P)
        x1 = sb("x1", [P, B, NJ, XA])
        blk_sum = sb("blk_sum", [NJ, B, D + 1])
        den = sb("den", [P, B, NJ])
        rden = sb("rden", [P, B, NJ])

        acc = [[bank(f"acc{d}{t}") for t in range(NT)] for d in range(KD)]
        gate_ps = bank("gate_ps")
        up_ps = bank("up_ps")
        spare = [bank(f"spare{i}") for i in range(2)]

        x_loaded = [[sem(f"x_loaded{b}{t}") for t in range(NT)] for b in range(B)]
        gates_loaded = sem("gates_loaded")
        l1_loaded = sem("l1_loaded")
        ones_ready = sem("ones_ready")
        ident_ready = sem("ident_ready")
        const_step = sem("const_step")
        gate_step = sem("gate_step")
        xT_done = sem("xT_done")
        xT_copied = sem("xT_copied")
        x_hi_done = sem("x_hi_done")
        x_split0 = sem("x_split0")
        x_hi1_done = sem("x_hi1_done")
        x_split1 = sem("x_split1")
        staged = [sem(f"staged{s}") for s in range(NSLOT)]
        gu_hi_done = sem("gu_hi_done")
        gu_split = sem("gu_split")
        d_hi_done = sem("d_hi_done")
        d_split = sem("d_split")
        gate_done = sem("gate_done")
        up_done = sem("up_done")
        silu_done = sem("silu_done")
        h_done = sem("h_done")
        h_hi_done = sem("h_hi_done")
        h_split = sem("h_split")
        down_done = sem("down_done")
        x1T_done = sem("x1T_done")
        attn_done = sem("attn_done")
        tanh_done = sem("tanh_done")
        x1_done = sem("x1_done")
        x1_copied = sem("x1_copied")
        score_done = sem("score_done")
        score_copied = sem("score_copied")
        self_copied = sem("self_copied")
        col_done = sem("col_done")
        col_copied = sem("col_copied")
        dve_l1 = sem("dve_l1")
        e_done = sem("e_done")
        carry_arg = sem("carry_arg")
        carry_done = sem("carry_done")
        prob_done = sem("prob_done")
        sum_done = sem("sum_done")
        sum_copied = sem("sum_copied")
        pool_done = sem("pool_done")
        out_done = sem("out_done")
        stored = sem("stored")

        MAXIMA = ("before0", "after0", "before", "after", "max1", "qmax", "parg")
        BLOCKS = ("blkmax", "diag", "blkcol", "earg")
        DVE_L1 = {}

        def dve_steps(b, *names):
            for name in names:
                DVE_L1[name, b] = len(DVE_L1) + 1

        HEAD = NB
        dve_steps(0, *MAXIMA, *BLOCKS, "ediag")
        dve_steps(0, *(f"{x}{j}" for j in range(HEAD) for x in ("den", "rden")))
        dve_steps(1, *BLOCKS, *MAXIMA[:4], "ediag", *MAXIMA[4:])
        dve_steps(0, *(f"{x}{j}" for j in range(HEAD, NJ) for x in ("den", "rden")))
        dve_steps(1, *(f"{x}{j}" for j in range(NJ) for x in ("den", "rden")))

        CONST_STEPS = 2 + 4 + 1 + 2 + 1 + 1 + 6 + 3 + 3 + B * (2 + 4 + 3 + 2)

        ATTN = spare
        X1 = [spare[1], spare[0]]
        SCORE = [spare, [gate_ps, up_ps]]
        COL = spare[0][:, 0:NJ]
        SUM = [ps[0:NJ, 0:D + 1] for ps in (gate_ps, up_ps)]
        POOLED = [acc[d][t] for t in range(NT) for d in range(KD)]

        block = ctx.enter_context(nc.Block())

        @block.sync
        def _(sp):
            def load_x(b, t):
                n = NJ // NT
                sp.dma_start(x_nat[:, b, t * n:(t + 1) * n, :], x_dram[b, t]).then_inc(x_loaded[b][t], 16)

            def load_slot(s, g, u, d, f0):
                for n, w in enumerate((g, u)):
                    sp.dma_start(raw_gu[:, s, n * KD:(n + 1) * KD, :],
                                 w[:, f0:f0 + SW].rearrange("(k p) f -> p k f", p=P)).then_inc(staged[s], 16)
                sp.dma_start(raw_d[:, s, :, :],
                             d[f0:f0 + SW, :].rearrange("(j p) d -> p j d", p=P)).then_inc(staged[s], 16)

            def load_expert(g, u, d, slot0, fresh=False):
                for n in range(HALVES * NSLOT):
                    if not (fresh and n < NSLOT):
                        sp.wait_ge(d_split, (slot0 + n - NSLOT + 1) * SLOT)
                    load_slot(n % NSLOT, g, u, d, n * SW)

            per = HALVES * NSLOT
            load_x(0, 0)
            load_slot(0, Wg[0], Wu[0], Wd[0], 0)
            load_x(0, 1)
            load_slot(1, Wg[0], Wu[0], Wd[0], SW)
            for t in range(NT):
                load_x(1, t)
            for n in range(NSLOT, per):
                sp.wait_ge(d_split, (n - NSLOT + 1) * SLOT)
                load_slot(n % NSLOT, Wg[0], Wu[0], Wd[0], n * SW)
            with sp.Fori(1, E) as e:
                load_expert(Wg[e], Wu[e], Wd[e], e * per)
            load_expert(Sg, Su, Sd, E * per)
            with sp.Fori(0, E) as e:
                load_expert(Wg[e], Wu[e], Wd[e], e * per + NEXP * per)
            load_expert(Sg, Su, Sd, (NEXP + E) * per)

            for b in range(B):
                for t in range(NT):
                    n = NJ // NT
                    sp.wait_ge(out_done, b * NJ + (t + 1) * n)
                    sp.dma_start(out_dram[b, t], x_nat[:, b, t * n:(t + 1) * n, :]).then_inc(stored, 16)
            sp.wait_ge(stored, 16 * B * NT)

        @block.gpsimd
        def _(pool):
            steps = [0]

            def const(ins):
                steps[0] += 1
                ins.then_inc(const_step, 1)
                pool.wait_ge(const_step, steps[0])

            nc.gpsimd.memset(zero[:], 0.0).then_inc(ones_ready, 1)
            nc.gpsimd.memset(ones[:], 1.0).then_inc(ones_ready, 1)
            pool.wait_ge(ones_ready, 2)
            nc.gpsimd.affine_select(out=ident[:], in_=ones[:], compare_op=ALU.is_equal, fill=0.0, base=0,
                                    pattern=[[1, P]], channel_multiplier=-1).then_inc(ident_ready, 1)

            def split_tile(f, step, first=False):
                s, j = f // SLOT, f % SLOT
                n = step * TILES + f
                if j == 0:
                    pool.wait_ge(staged[s], (step + 1) * 3 * 16)
                gu = raw_gu[:, s, :, j * P:(j + 1) * P]
                if not first:
                    pool.wait_ge(up_done, (n - TILES + 1) * NT)
                nc.gpsimd.tensor_tensor(wgu_hi[:, f, :, :], gu,
                                        zero[:, 0:1].unsqueeze(2).broadcast_to([P, 2 * KD, P]), ALU.add).then_inc(gu_hi_done, 1)
                pool.wait_ge(gu_hi_done, n + 1)
                nc.gpsimd.tensor_tensor(wgu_lo[:, f, :, :], gu, wgu_hi[:, f, :, :].bitcast(F32),
                                        ALU.subtract).then_inc(gu_split, 1)
                if not first:
                    pool.wait_ge(down_done, (n - TILES + 1) * NT)
                nc.gpsimd.tensor_tensor(wd_hi[:, f, :], raw_d[:, s, j, :], zero[:, 0:1].broadcast_to([P, D]),
                                        ALU.add).then_inc(d_hi_done, 1)
                pool.wait_ge(d_hi_done, n + 1)
                nc.gpsimd.tensor_tensor(wd_lo[:, f, :], raw_d[:, s, j, :], wd_hi[:, f, :].bitcast(F32),
                                        ALU.subtract).then_inc(d_split, 1)

            for f in range(TILES):
                split_tile(f, 0, first=True)

            pool.wait_ge(xT_copied, 2 * KD * NT)
            for k in range(KD):
                for t in range(NT):
                    half = slice(t * BANK, (t + 1) * BANK)
                    nc.gpsimd.tensor_copy(xT_hi[:, 1, k, half], xT[:, 1, k, half]).then_inc(x_hi1_done, 1)
                    pool.wait_ge(x_hi1_done, k * NT + t + 1)
                    nc.gpsimd.tensor_tensor(xT_lo[:, 1, k, half], xT[:, 1, k, half],
                                            xT_hi[:, 1, k, half].bitcast(F32), ALU.subtract).then_inc(x_split1, 1)

            def split_steps(first, end):
                with pool.Fori(first, end) as step:
                    for f in range(TILES):
                        split_tile(f, step)

            split_steps(1, 2)
            for m, sign in ((before, 1), (after, -1)):
                const(nc.gpsimd.affine_select(out=m[:], in_=ones[:], compare_op=ALU.is_gt, fill=0.0, base=0,
                                              pattern=[[sign, P]], channel_multiplier=-sign))
            for m, sign in ((blk_before, 1), (blk_after, -1)):
                const(nc.gpsimd.memset(m, 1.0))
                const(nc.gpsimd.affine_select(out=m, in_=m, compare_op=ALU.is_gt, fill=0.0, base=0,
                                              pattern=[[sign, NJ], [0, P]], channel_multiplier=-sign))
            const(nc.gpsimd.affine_select(out=eye[:], in_=ones[:, 0:NJ * NJ].rearrange("p (i j) -> p i j", j=NJ),
                                          compare_op=ALU.is_equal, fill=0.0, base=0,
                                          pattern=[[1, NJ], [-1, NJ]], channel_multiplier=0))
            const(nc.gpsimd.iota(pos_i[:], pattern=[[P, NJ]], base=0, channel_multiplier=1))
            const(nc.gpsimd.tensor_copy(pos[:], pos_i[:]))
            const(nc.gpsimd.memset(x1[:, :, :, D:XA], 1.0))

            split_steps(2, 3)
            pool.wait_ge(l1_loaded, 4 * 16)
            const(nc.gpsimd.tensor_scalar(v_rep[:], ones[0:A, :], v_sb[:, 0:1], None, ALU.mult))
            const(nc.gpsimd.tensor_copy(ptype[:], ptype_i[:]))
            const(nc.gpsimd.tensor_scalar(is_pre[:], ptype[:], 0.0, None, ALU.is_equal))
            const(nc.gpsimd.tensor_scalar(is_post[:], ptype[:], 1.0, None, ALU.is_equal))
            const(nc.gpsimd.tensor_scalar(w_before[:], is_post[:], -1.0, 1.0, ALU.mult, ALU.add))
            const(nc.gpsimd.tensor_scalar(w_after[:], is_pre[:], -1.0, 1.0, ALU.mult, ALU.add))
            const(nc.gpsimd.tensor_tensor(w_self[:], is_pre[:], is_post[:], ALU.add))
            for flag, w in ((f_before, w_before), (f_after, w_after), (f_self, w_self)):
                const(nc.gpsimd.tensor_scalar(flag[:], w[:], 1.0, -NEG_INF, ALU.subtract, ALU.mult))
            const(nc.gpsimd.tensor_tensor(cnt_slope[:], w_before[:], w_after[:], ALU.subtract))
            const(nc.gpsimd.tensor_scalar(cnt_rest[:], w_after[:], float(S - 1), None, ALU.mult))
            const(nc.gpsimd.tensor_tensor(cnt_rest[:], cnt_rest[:], w_self[:], ALU.add))

            for b in range(B):
                split_steps(3 + b, 4 + b)
                one = slice(b, b + 1)
                const(nc.gpsimd.tensor_scalar(cnt[:, b, :], pos[:], cnt_slope[:, one], cnt_rest[:, one],
                                              ALU.mult, ALU.add))
                const(nc.gpsimd.tensor_scalar(mask[:, b, :], ident[:], w_self[:, one], None, ALU.mult))
                for m, w in ((before, w_before), (after, w_after)):
                    const(nc.gpsimd.tensor_scalar(probT[:, b, 0, :], m[:], w[:, one], None, ALU.mult))
                    const(nc.gpsimd.tensor_tensor(mask[:, b, :], mask[:, b, :], probT[:, b, 0, :], ALU.add))
                const(nc.gpsimd.tensor_scalar(blk_mask[:, b], blk_before.rearrange("i j p -> i (j p)"),
                                              w_before[0:NJ, one], None, ALU.mult))
                const(nc.gpsimd.tensor_scalar(carry[:, b], blk_after.rearrange("i j p -> i (j p)"),
                                              w_after[0:NJ, one], None, ALU.mult))
                const(nc.gpsimd.tensor_tensor(blk_mask[:, b], blk_mask[:, b], carry[:, b], ALU.add))
                for m in (mask[:, b], blk_mask[:, b]):
                    const(nc.gpsimd.tensor_scalar(m, m, 1.0, -NEG_INF, ALU.subtract, ALU.mult))
            assert steps[0] == CONST_STEPS

            split_steps(3 + B, B * STEPS)

            for b in range(B):
                pool.wait_ge(dve_l1, DVE_L1["qmax", b])
                nc.gpsimd.tensor_tensor(carry[:, b], blk_mask[:, b], qmax[0:NJ, b, :],
                                        ALU.subtract).then_inc(carry_arg, 1)

        @block.scalar
        def _(act):
            act.dma_start(probs[:], fside.unsqueeze(0).broadcast_to([P, B, E])).then_inc(gates_loaded, 16)
            act.dma_start(sg[:], shared_gate.unsqueeze(0).broadcast_to([P, B])).then_inc(gates_loaded, 16)
            act.dma_start(ptype_i[:], prompt_type.unsqueeze(0).broadcast_to([P, B])).then_inc(l1_loaded, 16)
            act.dma_start(W1_sb[:], W1.rearrange("(k p) a -> p k a", p=P)).then_inc(l1_loaded, 16)
            act.dma_start(b1_sb[:], b1.unsqueeze(1)).then_inc(l1_loaded, 16)
            act.dma_start(v_sb[:], v.unsqueeze(1)).then_inc(l1_loaded, 16)

            for b in range(B):
                for t in range(NT):
                    for k in range(KD):
                        act.wait_ge(xT_done, (b * NT + t) * KD + k + 1)
                        nc.scalar.activation(xT[:, b, k, t * BANK:(t + 1) * BANK], acc[k][t][:],
                                             ACT.Copy).then_inc(xT_copied, 1)

            def silu(u, step):
                act.wait_ge(gate_done, step * UNITS + (u + 1))
                nc.scalar.activation(gate_silu[:, u % 2, :], gate_ps[:], ACT.Silu).then_inc(silu_done, 1)

            def tanh(b):
                for t in range(NT):
                    act.wait_ge(attn_done, b * NT + t + 1)
                    nc.scalar.activation(attnT[:, b, t * BANK:(t + 1) * BANK], ATTN[t][0:A, :], ACT.Tanh,
                                         bias=b1_sb[:, 0:1]).then_inc(tanh_done, 1)

            def copy_score(b):
                for t in range(NT):
                    half = slice(t * BANK, (t + 1) * BANK)
                    act.wait_ge(score_done, b * NT + t + 1)
                    nc.scalar.activation(score[:, b, half], SCORE[b][t][:], ACT.Copy).then_inc(score_copied, 1)
                for t in range(NT):
                    half = slice(t * BANK, (t + 1) * BANK)
                    nc.scalar.activation(score_self[:, b, half], SCORE[b][t][:], ACT.Identity,
                                         bias=f_self[:, b:b + 1]).then_inc(self_copied, 1)

            def copy_col(b):
                act.wait_ge(col_done, b + 1)
                nc.scalar.activation(score_col[:, b, :], COL, ACT.Copy).then_inc(col_copied, 1)

            def copy_x1(b, *banks):
                for n in banks:
                    act.wait_ge(x1_done, b * NB + n + 1)
                    nc.scalar.activation(x1[:, b, n * JB:(n + 1) * JB, 0:D],
                                         X1[n % 2][:].rearrange("p (j d) -> p j d", d=D),
                                         ACT.Copy).then_inc(x1_copied, 1)

            def exp_blocks(b):
                act.wait_ge(dve_l1, DVE_L1["earg", b])
                nc.scalar.activation(e_blk[:, b, :], e_blk[:, b, :], ACT.Exp).then_inc(e_done, 1)

            def copy_sum(b):
                act.wait_ge(sum_done, b + 1)
                nc.scalar.activation(blk_sum[:, b, :], SUM[b], ACT.Copy).then_inc(sum_copied, 1)

            def exp_carry(b):
                act.wait_ge(carry_arg, b + 1)
                act.wait_ge(dve_l1, DVE_L1["blkcol", b])
                nc.scalar.activation(carry[:, b, :], carry[:, b, :], ACT.Exp,
                                     bias=blk_max_col[:, b:b + 1]).then_inc(carry_done, 1)

            def exp_probs(b):
                act.wait_ge(dve_l1, DVE_L1["parg", b])
                act.wait_ge(col_copied, b + 1)
                for j in range(NJ):
                    nc.scalar.activation(probT[:, b, j, :], probT[:, b, j, :], ACT.Exp,
                                         bias=score_col[:, b, j:j + 1]).then_inc(prob_done, 1)

            with act.Fori(0, B * STEPS - 2) as step:
                for u in range(UNITS):
                    silu(u, step)
            for n in range(2 * UNITS):
                silu(n % UNITS, B * STEPS - 2 + n // UNITS)
                k = n - (2 * UNITS - LAST)
                if k == 0:
                    tanh(0)
                elif k == 1:
                    copy_score(0)
                elif k == 2:
                    copy_col(0)
                elif k == 3:
                    copy_x1(0, 0, 1)
                elif k == 4:
                    copy_x1(0, 2, 3)
            exp_blocks(0)
            exp_carry(0)
            exp_probs(0)
            copy_sum(0)
            tanh(1)
            copy_score(1)
            copy_x1(1, 0)
            copy_col(1)
            copy_x1(1, 1, 2, 3)
            exp_blocks(1)
            copy_sum(1)
            exp_carry(1)
            exp_probs(1)

        @block.vector
        def _(dve):
            dve.wait_ge(gates_loaded, 2 * 16)
            nc.vector.tensor_scalar(sg_rest[:], sg[:], -1.0, 1.0, ALU.mult, ALU.add).then_inc(gate_step, 1)
            dve.wait_ge(gate_step, 1)
            for b in range(B):
                for n in range(HALVES):
                    nc.vector.tensor_scalar(gates[:, b, 0:E, n], probs[:, b, :], sg_rest[:, b:b + 1], None,
                                            ALU.mult).then_inc(gate_step, 1)
                    nc.vector.tensor_copy(gates[:, b, E:NEXP, n], sg[:, b:b + 1]).then_inc(gate_step, 1)
            gate_of = gates[:].rearrange("p b e n -> p (b e n)")

            for t in range(NT):
                for k in range(KD):
                    n = t * KD + k + 1
                    half = slice(t * BANK, (t + 1) * BANK)
                    dve.wait_ge(xT_copied, n)
                    nc.vector.tensor_copy(xT_hi[:, 0, k, half], xT[:, 0, k, half]).then_inc(x_hi_done, 1)
                    dve.wait_ge(x_hi_done, n)
                    nc.vector.tensor_tensor(xT_lo[:, 0, k, half], xT[:, 0, k, half],
                                            xT_hi[:, 0, k, half].bitcast(F32), ALU.subtract).then_inc(x_split0, 1)
            dve.wait_ge(gate_step, 1 + 2 * B * HALVES)

            def hidden(u, step):
                n = step * UNITS + (u + 1)
                i, s = u % 2, u % HS
                dve.wait_ge(silu_done, n)
                dve.wait_ge(up_done, n)
                nc.vector.scalar_tensor_tensor(out=h[:, i, :], in0=gate_silu[:, i, :],
                                               scalar=gate_of[:, bass.ds(step, 1)], in1=up_ps[:],
                                               op0=ALU.mult, op1=ALU.mult).then_inc(h_done, 1)
                dve.wait_ge(h_done, n)
                nc.vector.tensor_copy(h_hi[:, s, :], h[:, i, :]).then_inc(h_hi_done, 1)
                dve.wait_ge(h_hi_done, n)
                nc.vector.tensor_tensor(h_lo[:, s, :], h[:, i, :], h_hi[:, s, :].bitcast(F32),
                                        ALU.subtract).then_inc(h_split, 1)

            def residual(b):
                dve.wait_ge(down_done, (b + 1) * UB)
                for t in range(NT):
                    for k in range(KD):
                        half = slice(t * BANK, (t + 1) * BANK)
                        nc.vector.tensor_tensor(xT[:, b, k, half], acc[k][t][:], xT[:, b, k, half],
                                                ALU.add).then_inc(x1T_done, 1)

            counted = [0]

            def step_done(name, b, ins):
                counted[0] += 1
                assert DVE_L1[name, b] == counted[0]
                ins.then_inc(dve_l1, 1)

            def after_step(name, b):
                dve.wait_ge(dve_l1, DVE_L1[name, b])

            def max_ends(b):
                step_done("before0", b, nc.vector.memset(max_before[:, b, 0:1], NEG_INF))
                step_done("after0", b, nc.vector.memset(qmax[:, b, S - 1:S], NEG_INF))

            def max_scan_before(b):
                sc = score[:, b, :]
                dve.wait_ge(score_copied, NT * (b + 1))
                step_done("before", b, nc.vector.tensor_tensor_scan(
                    max_before[:, b, 1:S], sc[:, 0:S - 1], sc[:, 0:S - 1], NEG_INF, ALU.max, ALU.max))

            def max_scan_after(b):
                sc = score[:, b, :]
                step_done("after", b, nc.vector.tensor_tensor_scan(
                    qmax[:, b, S - 2::-1], sc[:, S - 1:0:-1], sc[:, S - 1:0:-1], NEG_INF, ALU.max, ALU.max))

            def max_join_before(b):
                after_step("before", b)
                dve.wait_ge(self_copied, NT * (b + 1))
                step_done("max1", b, nc.vector.scalar_tensor_tensor(
                    out=score_self[:, b, :], in0=max_before[:, b, :], scalar=f_before[:, b:b + 1],
                    in1=score_self[:, b, :], op0=ALU.add, op1=ALU.max))

            def max_join_after(b):
                after_step("max1", b)
                step_done("qmax", b, nc.vector.scalar_tensor_tensor(
                    out=qmax[:, b, :], in0=qmax[:, b, :], scalar=f_after[:, b:b + 1],
                    in1=score_self[:, b, :], op0=ALU.add, op1=ALU.max))

            def prob_args(b):
                after_step("qmax", b)
                step_done("parg", b, nc.vector.tensor_tensor(
                    probT[:, b], mask[:, b, :].unsqueeze(1).broadcast_to([P, NJ, P]),
                    qmax[:, b, :].rearrange("p (j q) -> p j q", q=P), ALU.subtract))

            def block_maxima(b):
                dve.wait_ge(score_copied, NT * (b + 1))
                step_done("blkmax", b, nc.vector.tensor_reduce(
                    blk_max[:, b, :], score[:, b, :].rearrange("p (j l) -> p j l", l=P), AX_X, ALU.max))
                after_step("blkmax", b)
                step_done("diag", b, nc.vector.tensor_tensor(
                    blk_max_diag[:, b, :], blk_max[0:NJ, b, :], ident[0:NJ, 0:NJ], ALU.mult))
                after_step("diag", b)
                step_done("blkcol", b, nc.vector.tensor_reduce(
                    blk_max_col[:, b:b + 1], blk_max_diag[:, b, :], AX_X, ALU.add))
                dve.wait_ge(col_copied, b + 1)
                step_done("earg", b, nc.vector.tensor_tensor(
                    e_blk[:, b, :], score_col[:, b, :], blk_max[:, b, :], ALU.subtract))

            def block_weights(b):
                dve.wait_ge(e_done, b + 1)
                step_done("ediag", b, nc.vector.tensor_tensor(
                    e_diag[:, b], e_blk[:, b, :].unsqueeze(2).broadcast_to([P, NJ, NJ]), eye[:], ALU.mult))

            def finish(b, blocks):
                for j in blocks:
                    ps = POOLED[j % len(POOLED)]
                    dve.wait_ge(pool_done, b * NJ + j + 1)
                    step_done(f"den{j}", b, nc.vector.tensor_tensor(den[:, b, j:j + 1], ps[:, D:D + 1],
                                                                    cnt[:, b, j:j + 1], ALU.mult))
                    after_step(f"den{j}", b)
                    step_done(f"rden{j}", b, nc.vector.reciprocal(rden[:, b, j:j + 1], den[:, b, j:j + 1]))
                    after_step(f"rden{j}", b)
                    nc.vector.scalar_tensor_tensor(out=x_nat[:, b, j, :], in0=ps[:, 0:D],
                                                   scalar=rden[:, b, j:j + 1], in1=x1[:, b, j, 0:D],
                                                   op0=ALU.mult, op1=ALU.add).then_inc(out_done, 1)

            with dve.Fori(0, STEPS) as step:
                for u in range(UNITS):
                    hidden(u, step)
            hidden(0, STEPS)
            residual(0)
            for u in range(1, UNITS):
                hidden(u, STEPS)
            with dve.Fori(STEPS + 1, B * STEPS - 2) as step:
                for u in range(UNITS):
                    hidden(u, step)
            dve.wait_ge(const_step, CONST_STEPS)
            for n in range(2 * UNITS):
                hidden(n % UNITS, B * STEPS - 2 + n // UNITS)
                k = n - (2 * UNITS - LAST)
                if k == 1:
                    max_ends(0)
                elif k == 2:
                    max_scan_before(0)
                elif k == 3:
                    max_scan_after(0)
                elif k == 4:
                    max_join_before(0)
                elif k == 5:
                    max_join_after(0)
                elif k == 6:
                    prob_args(0)
                elif k == 7:
                    block_maxima(0)
            block_weights(0)
            residual(1)
            finish(0, range(HEAD))
            block_maxima(1)
            max_ends(1)
            max_scan_before(1)
            max_scan_after(1)
            block_weights(1)
            max_join_before(1)
            max_join_after(1)
            prob_args(1)
            finish(0, range(HEAD, NJ))
            finish(1, range(NJ))

        @block.tensor
        def _(pe):
            def transpose_x(b):
                n = NJ // NT
                for t in range(NT):
                    pe.wait_ge(x_loaded[b][t], 16)
                    for k in range(KD):
                        if b:
                            pe.wait_ge(xT_copied, ((b - 1) * NT + t) * KD + k + 1)
                        for j in range(n):
                            last = nc.tensor.transpose(acc[k][t][:, j * P:(j + 1) * P],
                                                       x_nat[:, b, t * n + j, k * P:(k + 1) * P], ident[:])
                        last.then_inc(xT_done, 1)

            def three_pass(ps, w_hi, w_lo, a_hi, a_lo, start, stop):
                nc.tensor.matmul(ps, w_hi, a_hi, start=start, stop=False)
                nc.tensor.matmul(ps, w_hi, a_lo, start=False, stop=False)
                return nc.tensor.matmul(ps, w_lo, a_hi, start=False, stop=stop)

            def project(ps, w0, b, u, first=False):
                f, t = u // NT, u % NT
                half = slice(t * BANK, (t + 1) * BANK)
                for k in range(KD):
                    if first:
                        pe.wait_ge(x_split0, k + 1)
                    mm = three_pass(ps[:], wgu_hi[:, f, w0 + k, :], wgu_lo[:, f, w0 + k, :],
                                    xT_hi[:, b, k, half], xT_lo[:, b, k, half], k == 0, k == KD - 1)
                return mm

            def gate(b, u, step, first=False):
                if u % NT == 0:
                    pe.wait_ge(gu_split, step * TILES + (u // NT + 1))
                if not first:
                    pe.wait_ge(silu_done, step * UNITS + u)
                project(gate_ps, 0, b, u, first).then_inc(gate_done, 1)

            def up(b, u, step, first=False):
                if not first:
                    pe.wait_ge(h_done, step * UNITS + u)
                project(up_ps, KD, b, u).then_inc(up_done, 1)

            def down(u, step, start=False, stop=False):
                f, t = u // NT, u % NT
                if t == 0:
                    pe.wait_ge(d_split, step * TILES + (f + 1))
                pe.wait_ge(h_split, step * UNITS + (u + 1))
                for d in range(KD):
                    cols = slice(d * P, (d + 1) * P)
                    mm = three_pass(acc[d][t][:], wd_hi[:, f, cols], wd_lo[:, f, cols],
                                    h_hi[:, u % HS, :], h_lo[:, u % HS, :], start, stop)
                mm.then_inc(down_done, 1)

            def unit(b, u, step):
                gate(b, u, step)
                down((u - LAG) % UNITS, step if u >= LAG else step - 1)
                up(b, u, step)

            def attn(b):
                for t in range(NT):
                    for k in range(KD):
                        mm = nc.tensor.matmul(ATTN[t][0:A, :], W1_sb[:, k, :],
                                              xT[:, b, k, t * BANK:(t + 1) * BANK], start=k == 0, stop=k == KD - 1)
                    mm.then_inc(attn_done, 1)

            def score_row(b):
                for t in range(NT):
                    pe.wait_ge(tanh_done, b * NT + t + 1)
                    nc.tensor.matmul(SCORE[b][t][:], v_rep[:], attnT[:, b, t * BANK:(t + 1) * BANK],
                                     start=True, stop=True).then_inc(score_done, 1)

            def score_cols(b):
                for j in range(NJ):
                    mm = nc.tensor.matmul(COL[:, j:j + 1], attnT[:, b, j * P:(j + 1) * P], v_sb[:, 0:1],
                                          start=True, stop=True)
                mm.then_inc(col_done, 1)

            def transpose_x1(b, *banks):
                for n in banks:
                    if n >= 2:
                        pe.wait_ge(x1_copied, b * NB + n - 1)
                    for j in range(JB):
                        for k in range(KD):
                            tok = (n * JB + j) * P
                            mm = nc.tensor.transpose(X1[n % 2][:, j * D + k * P:j * D + (k + 1) * P],
                                                     xT[:, b, k, tok:tok + P], ident[:])
                    mm.then_inc(x1_done, 1)

            def block_sums(b):
                pe.wait_ge(dve_l1, DVE_L1["ediag", b])
                pe.wait_ge(x1_copied, NB * (b + 1))
                for j in range(NJ):
                    mm = nc.tensor.matmul(SUM[b], e_diag[:, b, j, :], x1[:, b, j, 0:D + 1],
                                          start=j == 0, stop=j == NJ - 1)
                mm.then_inc(sum_done, 1)

            def pooled(b, blocks):
                pe.wait_ge(sum_copied, b + 1)
                pe.wait_ge(carry_done, b + 1)
                for j in blocks:
                    n = b * NJ + j
                    if n >= len(POOLED):
                        pe.wait_ge(out_done, n - len(POOLED) + 1)
                    pe.wait_ge(prob_done, n + 1)
                    ps = POOLED[j % len(POOLED)][:, 0:D + 1]
                    nc.tensor.matmul(ps, probT[:, b, j, :], x1[:, b, j, 0:D + 1], start=True, stop=False)
                    nc.tensor.matmul(ps, carry[:, b, j * P:(j + 1) * P], blk_sum[:, b, :],
                                     start=False, stop=True).then_inc(pool_done, 1)

            pe.wait_ge(ident_ready, 1)
            transpose_x(0)
            gate(0, 0, 0, first=True)
            up(0, 0, 0, first=True)
            transpose_x(1)
            pe.wait_ge(x_split0, KD * NT)
            gate(0, 1, 0)
            up(0, 1, 0)
            for b in range(B):
                s0 = b * STEPS
                for u in range(LAG, 2 * LAG):
                    gate(b, u, s0)
                    if b == 0:
                        pe.wait_ge(xT_copied, B * KD * NT)
                    else:
                        pe.wait_ge(x1T_done, KD * (u - LAG + 1))
                    down(u - LAG, s0, start=True)
                    up(b, u, s0)
                steps = STEPS - 1 if b + 1 < B else STEPS - 2
                with pe.Fori(s0, s0 + steps) as step:
                    for u in range(2 * LAG, UNITS):
                        unit(b, u, step)
                    for u in range(2 * LAG):
                        unit(b, u, step + 1)
                if b + 1 < B:
                    last = s0 + STEPS - 1
                    for u in range(2 * LAG, UNITS):
                        unit(b, u, last)
                    pe.wait_ge(x_split1, KD * NT)
                    for u in range(LAG):
                        gate(b + 1, u, last + 1)
                        down(UNITS - LAG + u, last, stop=True)
                        up(b + 1, u, last + 1)

            pe.wait_ge(const_step, CONST_STEPS)
            for k in range(LAST):
                n = B * UB - LAST + k
                unit(1, n % UNITS, n // UNITS)
                if k == 0:
                    attn(0)
                elif k == 1:
                    score_row(0)
                elif k == 2:
                    pe.wait_ge(score_copied, NT)
                    pe.wait_ge(self_copied, NT)
                    score_cols(0)
                elif k == 3:
                    pe.wait_ge(col_copied, 1)
                    transpose_x1(0, 0, 1)
                elif k == 4:
                    transpose_x1(0, 2, 3)
            down(UNITS - 2, B * STEPS - 1, stop=True)
            block_sums(0)
            down(UNITS - 1, B * STEPS - 1, stop=True)

            pe.wait_ge(x1T_done, B * KD * NT)
            attn(1)
            pooled(0, range(2))
            score_row(1)
            transpose_x1(1, 0)
            score_cols(1)
            pooled(0, range(2, HEAD))
            pe.wait_ge(col_copied, 2)
            transpose_x1(1, 1, 2, 3)
            pooled(0, range(HEAD, NJ - 2))
            pe.wait_ge(self_copied, B * NT)
            block_sums(1)
            pooled(0, range(NJ - 2, NJ))
            pooled(1, range(NJ))


_INS = ["x", "fside_Bx8_0", "condB_sharedgateprob", "itok_B_0_2", "L0_cond_Wg", "L0_cond_Wu", "L0_cond_Wd",
        "L0_cond_Sg", "L0_cond_Su", "L0_cond_Sd", "L1_cond_W1", "L1_cond_b1", "L1_cond_v"]


def kernel(**inputs):
    import numpy as np
    import concourse.bacc as bacc
    from concourse.bass_utils import run_bass_kernel_spmd

    nc = bacc.Bacc("TRN2", target_bir_lowering=False, num_devices=1)
    arrays, args = {}, []
    for name in _INS:
        a = np.ascontiguousarray(inputs[name])
        arrays[f"in_{name}"] = a
        args.append(nc.dram_tensor(f"in_{name}", a.shape, mybir.dt.from_np(a.dtype), kind="ExternalInput").ap())
    args.append(nc.dram_tensor("out_x", inputs["x"].shape, F32, kind="ExternalOutput").ap())
    cond_resid_kernel(nc, *args)
    return run_bass_kernel_spmd(nc, [arrays], core_ids=[0]).results[0]["out_x"]
```

```python
from contextlib import ExitStack

import concourse.bass as bass
from concourse import mybir

F32 = mybir.dt.float32
F32R = mybir.dt.float32r
I32 = mybir.dt.int32
ALU = mybir.AluOpType
ACT = mybir.ActivationFunctionType
AX_X = mybir.AxisListType.X

P = 128
BANK = 512
NEG_INF = -1e30


def cond_resid_kernel(nc, x, fside, shared_gate, prompt_type, Wg, Wu, Wd, Sg, Su, Sd, W1, b1, v, out):
    B, S, D = x.shape
    E, _, F = Wg.shape
    A = W1.shape[1]
    KD = D // P
    NT = S // BANK
    NJ = S // P
    NEXP = E + 1
    TILES = 4
    STEPS = NEXP * F // (P * TILES)
    HALVES = F // (P * TILES)
    UNITS = TILES * NT
    UB = STEPS * UNITS
    SLOT = 2
    NSLOT = TILES // SLOT
    SW = SLOT * P
    LAG = 2
    HS = LAG
    LAST = UNITS + UNITS // 2
    JB = BANK // D
    NB = NJ // JB
    BUSY_BEFORE_X, BUSY_BEFORE_W = 9, 16
    PIECE = 2
    XA = D + 4

    x_dram = x.rearrange("b (h j p) d -> b h p j d", p=P, j=PIECE)
    out_dram = out.rearrange("b (h j p) d -> b h p j d", p=P, j=PIECE)

    with ExitStack() as ctx:
        def sb(name, shape, dt=F32):
            return ctx.enter_context(nc.sbuf_tensor(name, shape, dt))

        def bank(name):
            return ctx.enter_context(nc.psum_tensor(name, [P, BANK], F32))

        def sem(name):
            return ctx.enter_context(nc.semaphore(name))

        x_nat = sb("x_nat", [P, B, NJ, D])
        xT = sb("xT", [P, B, KD, S])
        xT_hi = sb("xT_hi", [P, B, KD, S], F32R)
        xT_lo = sb("xT_lo", [P, B, KD, S], F32R)
        raw_gu = sb("raw_gu", [P, NSLOT, 2 * KD, SW])
        raw_d = sb("raw_d", [P, NSLOT, SLOT, D])
        wgu_hi = sb("wgu_hi", [P, TILES, 2 * KD, P], F32R)
        wgu_lo = sb("wgu_lo", [P, TILES, 2 * KD, P], F32R)
        wd_hi = sb("wd_hi", [P, TILES, D], F32R)
        wd_lo = sb("wd_lo", [P, TILES, D], F32R)
        gate_silu = sb("gate_silu", [P, 2, BANK])
        h = sb("h", [P, 2, BANK])
        h_hi = sb("h_hi", [P, HS, BANK], F32R)
        h_lo = sb("h_lo", [P, HS, BANK], F32R)
        probs = sb("probs", [P, B, E])
        sg = sb("sg", [P, B])
        sg_rest = sb("sg_rest", [P, B])
        gates = sb("gates", [P, B, NEXP, HALVES])
        ptype_i = sb("ptype_i", [P, B], I32)
        ptype = sb("ptype", [P, B])
        is_pre = sb("is_pre", [P, B])
        is_post = sb("is_post", [P, B])
        w_before = sb("w_before", [P, B])
        w_after = sb("w_after", [P, B])
        w_self = sb("w_self", [P, B])
        f_before = sb("f_before", [P, B])
        f_after = sb("f_after", [P, B])
        f_self = sb("f_self", [P, B])
        W1_sb = sb("W1_sb", [P, KD, A])
        b1_sb = sb("b1_sb", [A, 1])
        v_sb = sb("v_sb", [A, 1])
        v_rep = sb("v_rep", [A, P])
        ones = sb("ones", [P, P])
        zero = sb("zero", [P, 1])
        warm = sb("warm", [P, 1])
        ident = sb("ident", [P, P])
        before = sb("before", [P, P])
        after = sb("after", [P, P])
        eye = sb("eye", [P, NJ, NJ])
        pos_i = sb("pos_i", [P, NJ], I32)
        pos = sb("pos", [P, NJ])
        mask = sb("mask", [P, B, P])
        blk_mask = sb("blk_mask", [NJ, B, S])
        cnt_rest = sb("cnt_rest", [P, B])
        cnt_slope = sb("cnt_slope", [P, B])
        cnt = sb("cnt", [P, B, NJ])
        attnT = sb("attnT", [A, B, S])
        score = sb("score", [P, B, S])
        score_self = sb("score_self", [P, B, S])
        max_before = sb("max_before", [P, B, S])
        qmax = sb("qmax", [P, B, S])
        score_col = sb("score_col", [P, B, NJ])
        blk_max = sb("blk_max", [P, B, NJ])
        blk_max_diag = sb("blk_max_diag", [NJ, B, NJ])
        blk_max_col = sb("blk_max_col", [NJ, B])
        e_blk = sb("e_blk", [P, B, NJ])
        e_diag = sb("e_diag", [P, B, NJ, NJ])
        carry = sb("carry", [NJ, B, S])
        blk_before, blk_after = (qmax[0:NJ, i, :].rearrange("i (j p) -> i j p", p=P) for i in range(2))
        probT = score_self[:].rearrange("p b (j q) -> p b j q", q=P)
        x1 = sb("x1", [P, B, NJ, XA])
        blk_sum = sb("blk_sum", [NJ, B, D + 1])
        den = sb("den", [P, B, NJ])
        rden = sb("rden", [P, B, NJ])

        acc = [[bank(f"acc{d}{t}") for t in range(NT)] for d in range(KD)]
        gate_ps = bank("gate_ps")
        up_ps = bank("up_ps")
        spare = [bank(f"spare{i}") for i in range(2)]

        x_loaded = [[sem(f"x_loaded{b}{i}") for i in range(NJ // PIECE)] for b in range(B)]
        gates_loaded = sem("gates_loaded")
        l1_loaded = sem("l1_loaded")
        ones_ready = sem("ones_ready")
        warm_done = sem("warm_done")
        ident_ready = sem("ident_ready")
        const_step = sem("const_step")
        gate_step = sem("gate_step")
        xT_done = sem("xT_done")
        xT_copied = sem("xT_copied")
        x_hi_done = sem("x_hi_done")
        x_split0 = sem("x_split0")
        x_hi1_done = sem("x_hi1_done")
        x_split1 = sem("x_split1")
        staged = [sem(f"staged{s}") for s in range(NSLOT)]
        g0_hi_done = sem("g0_hi_done")
        g0_split = sem("g0_split")
        gu_hi_done = sem("gu_hi_done")
        gu_split = sem("gu_split")
        d_hi_done = sem("d_hi_done")
        d_split = sem("d_split")
        gate_done = sem("gate_done")
        up_done = sem("up_done")
        silu_done = sem("silu_done")
        h_done = sem("h_done")
        h_hi_done = sem("h_hi_done")
        h_split = sem("h_split")
        down_done = sem("down_done")
        x1T_done = sem("x1T_done")
        attn_done = sem("attn_done")
        tanh_done = sem("tanh_done")
        x1_done = sem("x1_done")
        x1_copied = sem("x1_copied")
        score_done = sem("score_done")
        score_copied = sem("score_copied")
        self_copied = sem("self_copied")
        col_done = sem("col_done")
        col_ready = sem("col_ready")
        dve_l1 = sem("dve_l1")
        e_done = sem("e_done")
        carry_arg = sem("carry_arg")
        carry_done = sem("carry_done")
        prob_done = sem("prob_done")
        sum_done = sem("sum_done")
        sum_copied = sem("sum_copied")
        pool_done = sem("pool_done")
        out_done = sem("out_done")
        stored = sem("stored")

        MAXIMA = ("before0", "after0", "before", "after", "max1", "qmax", "parg")
        BLOCKS = ("blkmax", "diag", "blkcol", "earg")
        DVE_L1 = {}

        def dve_steps(b, *names):
            for name in names:
                DVE_L1[name, b] = len(DVE_L1) + 1

        HEAD = 2
        dve_steps(0, "before0", "after0", "colprod", *MAXIMA[2:], *BLOCKS, "ediag")
        dve_steps(0, *(f"{x}{j}" for j in range(HEAD) for x in ("den", "rden")))
        dve_steps(1, *BLOCKS, *MAXIMA[:4], "ediag", *MAXIMA[4:])
        dve_steps(0, *(f"{x}{j}" for j in range(HEAD, NJ) for x in ("den", "rden")))
        dve_steps(1, *(f"{x}{j}" for j in range(NJ) for x in ("den", "rden")))

        CONST_STEPS = 2 + 4 + 1 + 2 + 1 + 1 + 6 + 3 + 3 + B * (2 + 4 + 3 + 2)

        ATTN = spare
        X1 = [spare[1], spare[0]]
        SCORE = [spare, [acc[d][NT - 1] for d in range(KD)]]
        COL = spare[0][:, 0:NJ]
        SUM = [ps[0:NJ, 0:D + 1] for ps in (gate_ps, acc[0][NT - 1])]
        POOLED = [up_ps, gate_ps, *(acc[d][0] for d in range(KD))]

        block = ctx.enter_context(nc.Block())

        @block.sync
        def _(sp):
            def load_x(b, t):
                n = NJ // PIECE // NT
                for i in range(t * n, (t + 1) * n):
                    sp.dma_start(x_nat[:, b, i * PIECE:(i + 1) * PIECE, :], x_dram[b, i]).then_inc(x_loaded[b][i], 16)

            def load_slot(s, g, u, d, f0):
                for n, w in enumerate((g, u)):
                    sp.dma_start(raw_gu[:, s, n * KD:(n + 1) * KD, :],
                                 w[:, f0:f0 + SW].rearrange("(k p) f -> p k f", p=P)).then_inc(staged[s], 16)
                sp.dma_start(raw_d[:, s, :, :],
                             d[f0:f0 + SW, :].rearrange("(j p) d -> p j d", p=P)).then_inc(staged[s], 16)

            def load_expert(g, u, d, slot0, first=0):
                for n in range(first, per):
                    sp.wait_ge(d_split, (slot0 + n - NSLOT + 1) * SLOT)
                    load_slot(n % NSLOT, g, u, d, n * SW)

            per = HALVES * NSLOT
            load_x(0, 0)
            load_slot(0, Wg[0], Wu[0], Wd[0], 0)
            load_x(0, 1)
            load_slot(1, Wg[0], Wu[0], Wd[0], SW)
            for t in range(NT):
                load_x(1, t)
            sp.dma_start(ptype_i[:], prompt_type.unsqueeze(0).broadcast_to([P, B])).then_inc(l1_loaded, 16)
            sp.dma_start(W1_sb[:], W1.rearrange("(k p) a -> p k a", p=P)).then_inc(l1_loaded, 16)
            sp.dma_start(b1_sb[:], b1.unsqueeze(1)).then_inc(l1_loaded, 16)
            sp.dma_start(v_sb[:], v.unsqueeze(1)).then_inc(l1_loaded, 16)
            load_expert(Wg[0], Wu[0], Wd[0], 0, first=NSLOT)
            with sp.Fori(1, E) as e:
                load_expert(Wg[e], Wu[e], Wd[e], e * per)
            load_expert(Sg, Su, Sd, E * per)
            with sp.Fori(0, E) as e:
                load_expert(Wg[e], Wu[e], Wd[e], e * per + NEXP * per)
            load_expert(Sg, Su, Sd, (NEXP + E) * per)

            for b in range(B):
                for i in range(NJ // PIECE):
                    sp.wait_ge(out_done, b * NJ + (i + 1) * PIECE)
                    sp.dma_start(out_dram[b, i], x_nat[:, b, i * PIECE:(i + 1) * PIECE, :]).then_inc(stored, 16)
            sp.wait_ge(stored, 16 * B * NJ // PIECE)

        @block.gpsimd
        def _(pool):
            steps = [0]

            def const(ins):
                steps[0] += 1
                ins.then_inc(const_step, 1)
                pool.wait_ge(const_step, steps[0])

            nc.gpsimd.memset(zero[:], 0.0).then_inc(ones_ready, 1)
            nc.gpsimd.memset(ones[:], 1.0).then_inc(ones_ready, 1)
            pool.wait_ge(ones_ready, 2)
            nc.gpsimd.affine_select(out=ident[:], in_=ones[:], compare_op=ALU.is_equal, fill=0.0, base=0,
                                    pattern=[[1, P]], channel_multiplier=-1).then_inc(ident_ready, 1)

            def split_tile(f, step, first=False):
                s, j = f // SLOT, f % SLOT
                n = step * TILES + f
                if j == 0:
                    pool.wait_ge(staged[s], (step + 1) * 3 * 16)
                gu = raw_gu[:, s, :, j * P:(j + 1) * P]
                if not first:
                    pool.wait_ge(up_done, (n - TILES + 1) * NT)
                parts = (slice(0, KD), slice(KD, 2 * KD)) if first and f == 0 else (slice(0, 2 * KD),)
                for i, w in enumerate(parts):
                    hi_done, split = (g0_hi_done, g0_split) if i + 1 < len(parts) else (gu_hi_done, gu_split)
                    nc.gpsimd.tensor_tensor(wgu_hi[:, f, w, :], gu[:, w, :],
                                            zero[:, 0:1].unsqueeze(2).broadcast_to([P, w.stop - w.start, P]),
                                            ALU.add).then_inc(hi_done, 1)
                    pool.wait_ge(hi_done, n + 1)
                    nc.gpsimd.tensor_tensor(wgu_lo[:, f, w, :], gu[:, w, :], wgu_hi[:, f, w, :].bitcast(F32),
                                            ALU.subtract).then_inc(split, 1)
                if not first:
                    pool.wait_ge(down_done, (n - TILES + 1) * NT)
                nc.gpsimd.tensor_tensor(wd_hi[:, f, :], raw_d[:, s, j, :], zero[:, 0:1].broadcast_to([P, D]),
                                        ALU.add).then_inc(d_hi_done, 1)
                pool.wait_ge(d_hi_done, n + 1)
                nc.gpsimd.tensor_tensor(wd_lo[:, f, :], raw_d[:, s, j, :], wd_hi[:, f, :].bitcast(F32),
                                        ALU.subtract).then_inc(d_split, 1)

            for f in range(TILES):
                split_tile(f, 0, first=True)

            pool.wait_ge(xT_copied, 2 * KD * NT)
            for k in range(KD):
                for t in range(NT):
                    half = slice(t * BANK, (t + 1) * BANK)
                    nc.gpsimd.tensor_copy(xT_hi[:, 1, k, half], xT[:, 1, k, half]).then_inc(x_hi1_done, 1)
                    pool.wait_ge(x_hi1_done, k * NT + t + 1)
                    nc.gpsimd.tensor_tensor(xT_lo[:, 1, k, half], xT[:, 1, k, half],
                                            xT_hi[:, 1, k, half].bitcast(F32), ALU.subtract).then_inc(x_split1, 1)

            def split_steps(first, end):
                with pool.Fori(first, end) as step:
                    for f in range(TILES):
                        split_tile(f, step)

            split_steps(1, 2)
            for m, sign in ((before, 1), (after, -1)):
                const(nc.gpsimd.affine_select(out=m[:], in_=ones[:], compare_op=ALU.is_gt, fill=0.0, base=0,
                                              pattern=[[sign, P]], channel_multiplier=-sign))
            for m, sign in ((blk_before, 1), (blk_after, -1)):
                const(nc.gpsimd.memset(m, 1.0))
                const(nc.gpsimd.affine_select(out=m, in_=m, compare_op=ALU.is_gt, fill=0.0, base=0,
                                              pattern=[[sign, NJ], [0, P]], channel_multiplier=-sign))
            const(nc.gpsimd.affine_select(out=eye[:], in_=ones[:, 0:NJ * NJ].rearrange("p (i j) -> p i j", j=NJ),
                                          compare_op=ALU.is_equal, fill=0.0, base=0,
                                          pattern=[[1, NJ], [-1, NJ]], channel_multiplier=0))
            const(nc.gpsimd.iota(pos_i[:], pattern=[[P, NJ]], base=0, channel_multiplier=1))
            const(nc.gpsimd.tensor_copy(pos[:], pos_i[:]))
            const(nc.gpsimd.memset(x1[:, :, :, D:XA], 1.0))

            split_steps(2, 4)
            pool.wait_ge(l1_loaded, 4 * 16)
            const(nc.gpsimd.tensor_scalar(v_rep[:], ones[0:A, :], v_sb[:, 0:1], None, ALU.mult))
            const(nc.gpsimd.tensor_copy(ptype[:], ptype_i[:]))
            const(nc.gpsimd.tensor_scalar(is_pre[:], ptype[:], 0.0, None, ALU.is_equal))
            const(nc.gpsimd.tensor_scalar(is_post[:], ptype[:], 1.0, None, ALU.is_equal))
            const(nc.gpsimd.tensor_scalar(w_before[:], is_post[:], -1.0, 1.0, ALU.mult, ALU.add))
            const(nc.gpsimd.tensor_scalar(w_after[:], is_pre[:], -1.0, 1.0, ALU.mult, ALU.add))
            const(nc.gpsimd.tensor_tensor(w_self[:], is_pre[:], is_post[:], ALU.add))
            for flag, w in ((f_before, w_before), (f_after, w_after), (f_self, w_self)):
                const(nc.gpsimd.tensor_scalar(flag[:], w[:], 1.0, -NEG_INF, ALU.subtract, ALU.mult))
            const(nc.gpsimd.tensor_tensor(cnt_slope[:], w_before[:], w_after[:], ALU.subtract))
            const(nc.gpsimd.tensor_scalar(cnt_rest[:], w_after[:], float(S - 1), None, ALU.mult))
            const(nc.gpsimd.tensor_tensor(cnt_rest[:], cnt_rest[:], w_self[:], ALU.add))

            for b in range(B):
                split_steps(4 + 2 * b, 6 + 2 * b)
                one = slice(b, b + 1)
                const(nc.gpsimd.tensor_scalar(cnt[:, b, :], pos[:], cnt_slope[:, one], cnt_rest[:, one],
                                              ALU.mult, ALU.add))
                const(nc.gpsimd.tensor_scalar(mask[:, b, :], ident[:], w_self[:, one], None, ALU.mult))
                for m, w in ((before, w_before), (after, w_after)):
                    const(nc.gpsimd.tensor_scalar(probT[:, b, 0, :], m[:], w[:, one], None, ALU.mult))
                    const(nc.gpsimd.tensor_tensor(mask[:, b, :], mask[:, b, :], probT[:, b, 0, :], ALU.add))
                const(nc.gpsimd.tensor_scalar(blk_mask[:, b], blk_before.rearrange("i j p -> i (j p)"),
                                              w_before[0:NJ, one], None, ALU.mult))
                const(nc.gpsimd.tensor_scalar(carry[:, b], blk_after.rearrange("i j p -> i (j p)"),
                                              w_after[0:NJ, one], None, ALU.mult))
                const(nc.gpsimd.tensor_tensor(blk_mask[:, b], blk_mask[:, b], carry[:, b], ALU.add))
                for m in (mask[:, b], blk_mask[:, b]):
                    const(nc.gpsimd.tensor_scalar(m, m, 1.0, -NEG_INF, ALU.subtract, ALU.mult))
            assert steps[0] == CONST_STEPS

            split_steps(4 + 2 * B, B * STEPS)

            for b in range(B):
                pool.wait_ge(dve_l1, DVE_L1["qmax", b])
                nc.gpsimd.tensor_tensor(carry[:, b], blk_mask[:, b], qmax[0:NJ, b, :],
                                        ALU.subtract).then_inc(carry_arg, 1)

        @block.scalar
        def _(act):
            act.dma_start(probs[:], fside.unsqueeze(0).broadcast_to([P, B, E])).then_inc(gates_loaded, 16)
            act.dma_start(sg[:], shared_gate.unsqueeze(0).broadcast_to([P, B])).then_inc(gates_loaded, 16)
            act.wait_ge(ones_ready, 2)
            nc.scalar.activation(warm[:], zero[:], ACT.Silu).then_inc(warm_done, 1)

            def copy_xT(b):
                for t in range(NT):
                    for k in range(KD):
                        act.wait_ge(xT_done, (b * NT + t) * KD + k + 1)
                        nc.scalar.activation(xT[:, b, k, t * BANK:(t + 1) * BANK], acc[k][t][:],
                                             ACT.Copy).then_inc(xT_copied, 1)

            def silu(u, step):
                act.wait_ge(gate_done, step * UNITS + (u + 1))
                nc.scalar.activation(gate_silu[:, u % 2, :], gate_ps[:], ACT.Silu).then_inc(silu_done, 1)

            def tanh(b):
                for t in range(NT):
                    act.wait_ge(attn_done, b * NT + t + 1)
                    nc.scalar.activation(attnT[:, b, t * BANK:(t + 1) * BANK], ATTN[t][0:A, :], ACT.Tanh,
                                         bias=b1_sb[:, 0:1]).then_inc(tanh_done, 1)

            def copy_score(b):
                for t in range(NT):
                    half = slice(t * BANK, (t + 1) * BANK)
                    act.wait_ge(score_done, b * NT + t + 1)
                    nc.scalar.activation(score[:, b, half], SCORE[b][t][:], ACT.Copy).then_inc(score_copied, 1)
                for t in range(NT):
                    half = slice(t * BANK, (t + 1) * BANK)
                    nc.scalar.activation(score_self[:, b, half], SCORE[b][t][:], ACT.Identity,
                                         bias=f_self[:, b:b + 1]).then_inc(self_copied, 1)

            def copy_col(b):
                act.wait_ge(col_done, 1)
                nc.scalar.activation(score_col[:, b, :], COL, ACT.Copy).then_inc(col_ready, 1)

            def copy_x1(b, *banks):
                for n in banks:
                    act.wait_ge(x1_done, b * NB + n + 1)
                    nc.scalar.activation(x1[:, b, n * JB:(n + 1) * JB, 0:D],
                                         X1[n % 2][:].rearrange("p (j d) -> p j d", d=D),
                                         ACT.Copy).then_inc(x1_copied, 1)

            def exp_blocks(b):
                act.wait_ge(dve_l1, DVE_L1["earg", b])
                nc.scalar.activation(e_blk[:, b, :], e_blk[:, b, :], ACT.Exp).then_inc(e_done, 1)

            def copy_sum(b):
                act.wait_ge(sum_done, b + 1)
                nc.scalar.activation(blk_sum[:, b, :], SUM[b], ACT.Copy).then_inc(sum_copied, 1)

            def exp_carry(b):
                act.wait_ge(carry_arg, b + 1)
                act.wait_ge(dve_l1, DVE_L1["blkcol", b])
                nc.scalar.activation(carry[:, b, :], carry[:, b, :], ACT.Exp,
                                     bias=blk_max_col[:, b:b + 1]).then_inc(carry_done, 1)

            def exp_probs(b, blocks):
                act.wait_ge(dve_l1, DVE_L1["parg", b])
                act.wait_ge(col_ready, b + 1)
                for j in blocks:
                    nc.scalar.activation(probT[:, b, j, :], probT[:, b, j, :], ACT.Exp,
                                         bias=score_col[:, b, j:j + 1]).then_inc(prob_done, 1)

            copy_xT(0)
            silu(0, 0)
            copy_xT(1)
            for u in range(1, UNITS):
                silu(u, 0)
            with act.Fori(1, B * STEPS - 2) as step:
                for u in range(UNITS):
                    silu(u, step)
            for n in range(2 * UNITS):
                silu(n % UNITS, B * STEPS - 2 + n // UNITS)
                k = n - (2 * UNITS - LAST)
                if k == 0:
                    tanh(0)
                elif k == 1:
                    copy_score(0)
                elif k == 2:
                    copy_x1(0, 0, 1)
                elif k == 3:
                    copy_x1(0, 2, 3)
            exp_blocks(0)
            exp_carry(0)
            exp_probs(0, range(NJ))
            copy_sum(0)
            tanh(1)
            copy_score(1)
            copy_x1(1, 0)
            copy_col(1)
            copy_x1(1, 1, 2, 3)
            exp_blocks(1)
            copy_sum(1)
            exp_probs(1, range(HEAD))
            exp_carry(1)
            exp_probs(1, range(HEAD, NJ))

        @block.vector
        def _(dve):
            dve.wait_ge(gates_loaded, 2 * 16)
            nc.vector.tensor_scalar(sg_rest[:], sg[:], -1.0, 1.0, ALU.mult, ALU.add).then_inc(gate_step, 1)
            dve.wait_ge(gate_step, 1)
            for b in range(B):
                for n in range(HALVES):
                    nc.vector.tensor_scalar(gates[:, b, 0:E, n], probs[:, b, :], sg_rest[:, b:b + 1], None,
                                            ALU.mult).then_inc(gate_step, 1)
                    nc.vector.tensor_copy(gates[:, b, E:NEXP, n], sg[:, b:b + 1]).then_inc(gate_step, 1)
            gate_of = gates[:].rearrange("p b e n -> p (b e n)")

            for t in range(NT):
                for k in range(KD):
                    n = t * KD + k + 1
                    half = slice(t * BANK, (t + 1) * BANK)
                    dve.wait_ge(xT_copied, n)
                    nc.vector.tensor_copy(xT_hi[:, 0, k, half], xT[:, 0, k, half]).then_inc(x_hi_done, 1)
                    dve.wait_ge(x_hi_done, n)
                    nc.vector.tensor_tensor(xT_lo[:, 0, k, half], xT[:, 0, k, half],
                                            xT_hi[:, 0, k, half].bitcast(F32), ALU.subtract).then_inc(x_split0, 1)
            dve.wait_ge(gate_step, 1 + 2 * B * HALVES)

            def hidden(u, step):
                n = step * UNITS + (u + 1)
                i, s = u % 2, u % HS
                dve.wait_ge(silu_done, n)
                dve.wait_ge(up_done, n)
                nc.vector.scalar_tensor_tensor(out=h[:, i, :], in0=gate_silu[:, i, :],
                                               scalar=gate_of[:, bass.ds(step, 1)], in1=up_ps[:],
                                               op0=ALU.mult, op1=ALU.mult).then_inc(h_done, 1)
                dve.wait_ge(h_done, n)
                nc.vector.tensor_copy(h_hi[:, s, :], h[:, i, :]).then_inc(h_hi_done, 1)
                dve.wait_ge(h_hi_done, n)
                nc.vector.tensor_tensor(h_lo[:, s, :], h[:, i, :], h_hi[:, s, :].bitcast(F32),
                                        ALU.subtract).then_inc(h_split, 1)

            def residual(b):
                dve.wait_ge(down_done, (b + 1) * UB)
                for t in range(NT):
                    for k in range(KD):
                        half = slice(t * BANK, (t + 1) * BANK)
                        nc.vector.tensor_tensor(xT[:, b, k, half], acc[k][t][:], xT[:, b, k, half],
                                                ALU.add).then_inc(x1T_done, 1)

            counted = [0]

            def step_done(name, b, ins):
                counted[0] += 1
                assert DVE_L1[name, b] == counted[0]
                ins.then_inc(dve_l1, 1)

            def after_step(name, b):
                dve.wait_ge(dve_l1, DVE_L1[name, b])

            def max_ends(b):
                step_done("before0", b, nc.vector.memset(max_before[:, b, 0:1], NEG_INF))
                step_done("after0", b, nc.vector.memset(qmax[:, b, S - 1:S], NEG_INF))

            def max_scan_before(b):
                sc = score[:, b, :]
                dve.wait_ge(score_copied, NT * (b + 1))
                step_done("before", b, nc.vector.tensor_tensor_scan(
                    max_before[:, b, 1:S], sc[:, 0:S - 1], sc[:, 0:S - 1], NEG_INF, ALU.max, ALU.max))

            def max_scan_after(b):
                sc = score[:, b, :]
                step_done("after", b, nc.vector.tensor_tensor_scan(
                    qmax[:, b, S - 2::-1], sc[:, S - 1:0:-1], sc[:, S - 1:0:-1], NEG_INF, ALU.max, ALU.max))

            def max_join_before(b):
                after_step("before", b)
                dve.wait_ge(self_copied, NT * (b + 1))
                step_done("max1", b, nc.vector.scalar_tensor_tensor(
                    out=score_self[:, b, :], in0=max_before[:, b, :], scalar=f_before[:, b:b + 1],
                    in1=score_self[:, b, :], op0=ALU.add, op1=ALU.max))

            def max_join_after(b):
                after_step("max1", b)
                step_done("qmax", b, nc.vector.scalar_tensor_tensor(
                    out=qmax[:, b, :], in0=qmax[:, b, :], scalar=f_after[:, b:b + 1],
                    in1=score_self[:, b, :], op0=ALU.add, op1=ALU.max))

            def prob_args(b):
                after_step("qmax", b)
                step_done("parg", b, nc.vector.tensor_tensor(
                    probT[:, b], mask[:, b, :].unsqueeze(1).broadcast_to([P, NJ, P]),
                    qmax[:, b, :].rearrange("p (j q) -> p j q", q=P), ALU.subtract))

            def block_maxima(b):
                dve.wait_ge(score_copied, NT * (b + 1))
                step_done("blkmax", b, nc.vector.tensor_reduce(
                    blk_max[:, b, :], score[:, b, :].rearrange("p (j l) -> p j l", l=P), AX_X, ALU.max))
                after_step("blkmax", b)
                step_done("diag", b, nc.vector.tensor_tensor(
                    blk_max_diag[:, b, :], blk_max[0:NJ, b, :], ident[0:NJ, 0:NJ], ALU.mult))
                after_step("diag", b)
                step_done("blkcol", b, nc.vector.tensor_reduce(
                    blk_max_col[:, b:b + 1], blk_max_diag[:, b, :], AX_X, ALU.add))
                dve.wait_ge(col_ready, b + 1)
                step_done("earg", b, nc.vector.tensor_tensor(
                    e_blk[:, b, :], score_col[:, b, :], blk_max[:, b, :], ALU.subtract))

            def score_columns(b):
                prod = x_nat[:, b, :, 0:P]
                dve.wait_ge(score_copied, NT * (b + 1))
                step_done("colprod", b, nc.vector.tensor_tensor(
                    prod, score[:, b, :].rearrange("p (j l) -> p j l", l=P),
                    ident[:].unsqueeze(1).broadcast_to([P, NJ, P]), ALU.mult))
                after_step("colprod", b)
                nc.vector.tensor_reduce(score_col[:, b, :], prod, AX_X, ALU.add).then_inc(col_ready, 1)

            def block_weights(b):
                dve.wait_ge(e_done, b + 1)
                step_done("ediag", b, nc.vector.tensor_tensor(
                    e_diag[:, b], e_blk[:, b, :].unsqueeze(2).broadcast_to([P, NJ, NJ]), eye[:], ALU.mult))

            def finish(b, blocks):
                for j in blocks:
                    ps = POOLED[j % len(POOLED)]
                    dve.wait_ge(pool_done, b * NJ + j + 1)
                    step_done(f"den{j}", b, nc.vector.tensor_tensor(den[:, b, j:j + 1], ps[:, D:D + 1],
                                                                    cnt[:, b, j:j + 1], ALU.mult))
                    after_step(f"den{j}", b)
                    step_done(f"rden{j}", b, nc.vector.reciprocal(rden[:, b, j:j + 1], den[:, b, j:j + 1]))
                    after_step(f"rden{j}", b)
                    nc.vector.scalar_tensor_tensor(out=x_nat[:, b, j, :], in0=ps[:, 0:D],
                                                   scalar=rden[:, b, j:j + 1], in1=x1[:, b, j, 0:D],
                                                   op0=ALU.mult, op1=ALU.add).then_inc(out_done, 1)

            with dve.Fori(0, STEPS) as step:
                for u in range(UNITS):
                    hidden(u, step)
            hidden(0, STEPS)
            residual(0)
            for u in range(1, UNITS):
                hidden(u, STEPS)
            with dve.Fori(STEPS + 1, B * STEPS - 2) as step:
                for u in range(UNITS):
                    hidden(u, step)
            dve.wait_ge(const_step, CONST_STEPS)
            for n in range(2 * UNITS):
                if n == 2 * UNITS - 1:
                    block_weights(0)
                hidden(n % UNITS, B * STEPS - 2 + n // UNITS)
                k = n - (2 * UNITS - LAST)
                if k == 1:
                    max_ends(0)
                elif k == 2:
                    score_columns(0)
                elif k == 3:
                    max_scan_before(0)
                elif k == 4:
                    max_scan_after(0)
                elif k == 5:
                    max_join_before(0)
                elif k == 6:
                    max_join_after(0)
                elif k == 7:
                    prob_args(0)
                elif k == 8:
                    block_maxima(0)
            residual(1)
            finish(0, range(HEAD))
            block_maxima(1)
            max_ends(1)
            max_scan_before(1)
            max_scan_after(1)
            block_weights(1)
            max_join_before(1)
            max_join_after(1)
            prob_args(1)
            finish(0, range(HEAD, NJ))
            finish(1, range(NJ))

        @block.tensor
        def _(pe):
            def transpose_x(b, *halves):
                n = NJ // NT
                for t in halves:
                    for k in range(KD):
                        if b:
                            pe.wait_ge(xT_copied, ((b - 1) * NT + t) * KD + k + 1)
                        for j in range(n):
                            if k == 0 and j % PIECE == 0:
                                pe.wait_ge(x_loaded[b][(t * n + j) // PIECE], 16)
                            last = nc.tensor.transpose(acc[k][t][:, j * P:(j + 1) * P],
                                                       x_nat[:, b, t * n + j, k * P:(k + 1) * P], ident[:])
                        last.then_inc(xT_done, 1)

            def keep_busy(n):
                for _ in range(n):
                    nc.tensor.transpose(spare[0][:, 0:P], ident[:], ident[:])

            def three_pass(ps, w_hi, w_lo, a_hi, a_lo, start, stop, lo_ready=None):
                nc.tensor.matmul(ps, w_hi, a_hi, start=start, stop=False)
                nc.tensor.matmul(ps, w_lo, a_hi, start=False, stop=False)
                if lo_ready is not None:
                    pe.wait_ge(*lo_ready)
                return nc.tensor.matmul(ps, w_hi, a_lo, start=False, stop=stop)

            def project(ps, w0, b, u, first=False):
                f, t = u // NT, u % NT
                half = slice(t * BANK, (t + 1) * BANK)
                for k in range(KD):
                    if first:
                        pe.wait_ge(x_hi_done, k + 1)
                    mm = three_pass(ps[:], wgu_hi[:, f, w0 + k, :], wgu_lo[:, f, w0 + k, :],
                                    xT_hi[:, b, k, half], xT_lo[:, b, k, half], k == 0, k == KD - 1,
                                    (x_split0, k + 1) if first else None)
                return mm

            def gate(b, u, step, first=False):
                if first:
                    pe.wait_ge(g0_split, 1)
                elif u % NT == 0:
                    pe.wait_ge(gu_split, step * TILES + (u // NT + 1))
                if not first:
                    pe.wait_ge(silu_done, step * UNITS + u)
                project(gate_ps, 0, b, u, first).then_inc(gate_done, 1)

            def up(b, u, step, first=False):
                if first:
                    pe.wait_ge(gu_split, 1)
                else:
                    pe.wait_ge(h_done, step * UNITS + u)
                project(up_ps, KD, b, u).then_inc(up_done, 1)

            def down(u, step, start=False, stop=False):
                f, t = u // NT, u % NT
                if t == 0:
                    pe.wait_ge(d_split, step * TILES + (f + 1))
                pe.wait_ge(h_split, step * UNITS + (u + 1))
                for d in range(KD):
                    cols = slice(d * P, (d + 1) * P)
                    mm = three_pass(acc[d][t][:], wd_hi[:, f, cols], wd_lo[:, f, cols],
                                    h_hi[:, u % HS, :], h_lo[:, u % HS, :], start, stop)
                mm.then_inc(down_done, 1)

            def unit(b, u, step):
                gate(b, u, step)
                down((u - LAG) % UNITS, step if u >= LAG else step - 1)
                up(b, u, step)

            def attn(b):
                for t in range(NT):
                    pe.wait_ge(x1T_done, (b * NT + t + 1) * KD)
                    for k in range(KD):
                        mm = nc.tensor.matmul(ATTN[t][0:A, :], W1_sb[:, k, :],
                                              xT[:, b, k, t * BANK:(t + 1) * BANK], start=k == 0, stop=k == KD - 1)
                    mm.then_inc(attn_done, 1)

            def score_row(b):
                for t in range(NT):
                    pe.wait_ge(tanh_done, b * NT + t + 1)
                    nc.tensor.matmul(SCORE[b][t][:], v_rep[:], attnT[:, b, t * BANK:(t + 1) * BANK],
                                     start=True, stop=True).then_inc(score_done, 1)

            def score_cols(b):
                for j in range(NJ):
                    mm = nc.tensor.matmul(COL[:, j:j + 1], attnT[:, b, j * P:(j + 1) * P], v_sb[:, 0:1],
                                          start=True, stop=True)
                mm.then_inc(col_done, 1)

            def transpose_x1(b, *banks):
                for n in banks:
                    if n >= 2:
                        pe.wait_ge(x1_copied, b * NB + n - 1)
                    for j in range(JB):
                        for k in range(KD):
                            tok = (n * JB + j) * P
                            mm = nc.tensor.transpose(X1[n % 2][:, j * D + k * P:j * D + (k + 1) * P],
                                                     xT[:, b, k, tok:tok + P], ident[:])
                    mm.then_inc(x1_done, 1)

            def block_sums(b):
                pe.wait_ge(dve_l1, DVE_L1["ediag", b])
                pe.wait_ge(x1_copied, NB * (b + 1))
                for j in range(NJ):
                    mm = nc.tensor.matmul(SUM[b], e_diag[:, b, j, :], x1[:, b, j, 0:D + 1],
                                          start=j == 0, stop=j == NJ - 1)
                mm.then_inc(sum_done, 1)

            def pooled(b, blocks):
                for j in blocks:
                    n = b * NJ + j
                    if n >= len(POOLED):
                        pe.wait_ge(out_done, n - len(POOLED) + 1)
                    pe.wait_ge(prob_done, n + 1)
                    nc.tensor.matmul(POOLED[j % len(POOLED)][:, 0:D + 1], probT[:, b, j, :], x1[:, b, j, 0:D + 1],
                                     start=True, stop=False)
                pe.wait_ge(sum_copied, b + 1)
                pe.wait_ge(carry_done, b + 1)
                for j in blocks:
                    nc.tensor.matmul(POOLED[j % len(POOLED)][:, 0:D + 1], carry[:, b, j * P:(j + 1) * P],
                                     blk_sum[:, b, :], start=False, stop=True).then_inc(pool_done, 1)

            pe.wait_ge(ident_ready, 1)
            keep_busy(BUSY_BEFORE_X)
            transpose_x(0, 0)
            keep_busy(BUSY_BEFORE_W)
            gate(0, 0, 0, first=True)
            transpose_x(0, 1)
            up(0, 0, 0, first=True)
            transpose_x(1, *range(NT))
            pe.wait_ge(x_split0, KD * NT)
            gate(0, 1, 0)
            up(0, 1, 0)
            for b in range(B):
                s0 = b * STEPS
                for u in range(LAG, 2 * LAG):
                    gate(b, u, s0)
                    if b == 0:
                        pe.wait_ge(xT_copied, B * KD * NT)
                    else:
                        pe.wait_ge(x1T_done, KD * (u - LAG + 1))
                    down(u - LAG, s0, start=True)
                    up(b, u, s0)
                steps = STEPS - 1 if b + 1 < B else STEPS - 2
                with pe.Fori(s0, s0 + steps) as step:
                    for u in range(2 * LAG, UNITS):
                        unit(b, u, step)
                    for u in range(2 * LAG):
                        unit(b, u, step + 1)
                if b + 1 < B:
                    last = s0 + STEPS - 1
                    for u in range(2 * LAG, UNITS):
                        unit(b, u, last)
                    pe.wait_ge(x_split1, KD * NT)
                    for u in range(LAG):
                        gate(b + 1, u, last + 1)
                        down(UNITS - LAG + u, last, stop=True)
                        up(b + 1, u, last + 1)

            pe.wait_ge(const_step, CONST_STEPS)
            for k in range(LAST):
                n = B * UB - LAST + k
                unit(1, n % UNITS, n // UNITS)
                if k == 0:
                    attn(0)
                elif k == 1:
                    score_row(0)
                elif k == 2:
                    pe.wait_ge(score_copied, NT)
                    pe.wait_ge(self_copied, NT)
                    transpose_x1(0, 0, 1)
                elif k == 3:
                    transpose_x1(0, 2, 3)
            down(UNITS - 2, B * STEPS - 1, stop=True)
            block_sums(0)
            down(UNITS - 1, B * STEPS - 1, stop=True)

            pe.wait_ge(sum_copied, 1)
            pooled(0, range(HEAD))
            attn(1)
            pooled(0, range(HEAD, HEAD + 1))
            score_row(1)
            transpose_x1(1, 0)
            score_cols(1)
            pooled(0, range(HEAD + 1, len(POOLED)))
            pe.wait_ge(col_ready, 2)
            transpose_x1(1, 1, 2, 3)
            pooled(0, range(len(POOLED), len(POOLED) + HEAD))
            pe.wait_ge(self_copied, B * NT)
            block_sums(1)
            pooled(0, range(len(POOLED) + HEAD, NJ))
            for j in range(0, NJ, HEAD):
                pooled(1, range(j, j + HEAD))


_INS = ["x", "fside_Bx8_0", "condB_sharedgateprob", "itok_B_0_2", "L0_cond_Wg", "L0_cond_Wu", "L0_cond_Wd",
        "L0_cond_Sg", "L0_cond_Su", "L0_cond_Sd", "L1_cond_W1", "L1_cond_b1", "L1_cond_v"]


def kernel(**inputs):
    import numpy as np
    import concourse.bacc as bacc
    from concourse.bass_utils import run_bass_kernel_spmd

    nc = bacc.Bacc("TRN2", target_bir_lowering=False, num_devices=1)
    arrays, args = {}, []
    for name in _INS:
        a = np.ascontiguousarray(inputs[name])
        arrays[f"in_{name}"] = a
        args.append(nc.dram_tensor(f"in_{name}", a.shape, mybir.dt.from_np(a.dtype), kind="ExternalInput").ap())
    args.append(nc.dram_tensor("out_x", inputs["x"].shape, F32, kind="ExternalOutput").ap())
    cond_resid_kernel(nc, *args)
    return run_bass_kernel_spmd(nc, [arrays], core_ids=[0]).results[0]["out_x"]
```
